# Optimizing a Trainium2 kernel written in Bass

```python
import numpy as np
import jax
import jax.numpy as jnp

def _softmax(x, axis=-1):
    return jax.nn.softmax(x, axis=axis)

def _gelu(x):
    return jax.nn.gelu(x, approximate=True)

def _silu(x):
    return jax.nn.silu(x)

def _sigmoid(x):
    return jax.nn.sigmoid(x)

def _layernorm(x, axis=-1, eps=1e-05):
    m = jnp.mean(x, axis=axis, keepdims=True)
    v = jnp.var(x, axis=axis, keepdims=True)
    return (x - m) / jnp.sqrt(v + eps)

def _scatter_add(tgt, idx, src, axis=0):
    return tgt.at[idx].add(src)

def _segment_sum(src, seg, n):
    return jax.ops.segment_sum(src, seg, n)
kernel_name = 'mk_gnn_resnorm_d4_gnn_r8_1d918b'

def setup_inputs(seed: int=0):
    np.random.seed(seed)
    _w = jnp.asarray

    def _rec_inputs():
        import jax
        import jax.numpy as jnp
        _gk = jax.random.key(seed)
        x = -0.000202 + 1 * jax.random.normal(jax.random.fold_in(_gk, 1), (12500, 64), jnp.float32)
        src = jax.random.randint(jax.random.fold_in(_gk, 2), (200000,), 0, 12500, jnp.int32)
        dst = jax.random.randint(jax.random.fold_in(_gk, 3), (200000,), 0, 12500, jnp.int32)
        _o = jnp.argsort(dst, stable=True)
        src = src[_o]
        dst = dst[_o]
        edge_attr_32 = 0.000216709 + 1.00012 * jax.random.normal(jax.random.fold_in(_gk, 12), (200000, 32), jnp.float32)
        edge_type_16 = jax.random.randint(jax.random.fold_in(_gk, 14), (200000,), 0, 16, jnp.int32)
        return (x, src, dst, edge_attr_32, edge_type_16)
    x, src, dst, edge_attr_32, edge_type_16 = _rec_inputs()

    def _L0_gnn_setup():
        import jax, jax.numpy as jnp
        import numpy as np
        N_NODES = 12500
        N_EDGES = 200000
        IN_DIM = 64
        HIDDEN = 256
        OUT_DIM = 64
        key = jax.random.key(seed)
        ks = jax.random.split(key, 6)
        x = jax.random.normal(ks[0], (N_NODES, IN_DIM), dtype=jnp.float32)
        edge_index = jax.random.randint(ks[1], (2, N_EDGES), 0, N_NODES, dtype=jnp.int64)
        W1 = jax.random.normal(ks[2], (IN_DIM, HIDDEN), dtype=jnp.float32) / np.sqrt(IN_DIM)
        b1 = jnp.zeros((HIDDEN,), dtype=jnp.float32)
        W2 = jax.random.normal(ks[3], (HIDDEN, OUT_DIM), dtype=jnp.float32) / np.sqrt(HIDDEN)
        b2 = jnp.zeros((OUT_DIM,), dtype=jnp.float32)
        return {'x': x, 'edge_index': edge_index, 'W1': W1, 'b1': b1, 'W2': W2, 'b2': b2}
    _L0_gnn_all = _L0_gnn_setup()
    _L0_gnn_in = {k: v for k, v in _L0_gnn_all.items() if k in ('W1', 'b1', 'W2', 'b2')}
    del _L0_gnn_all

    def _L1_gnn_setup():
        import jax, jax.numpy as jnp
        import numpy as np
        N_NODES = 6250
        N_EDGES = 100000
        D_NODE = 64
        D_EDGE = 32
        D_HID = 128

        def _mlp(x, W1, b1, W2, b2):
            return jax.nn.relu(x @ W1 + b1) @ W2 + b2
        key = jax.random.key(seed)
        ks = jax.random.split(key, 12)
        inp = {'nodes': jax.random.normal(ks[0], (N_NODES, D_NODE), dtype=jnp.float32), 'row': jax.random.randint(ks[1], (N_EDGES,), 0, N_NODES, dtype=jnp.int32), 'col': jax.random.randint(ks[2], (N_EDGES,), 0, N_NODES, dtype=jnp.int32), 'edge_features': jax.random.normal(ks[3], (N_EDGES, D_EDGE), dtype=jnp.float32)}
        d_in_msg = 2 * D_NODE + D_EDGE
        inp['mW1'] = jax.random.normal(ks[4], (d_in_msg, D_HID), dtype=jnp.float32) / np.sqrt(d_in_msg)
        inp['mb1'] = jnp.zeros((D_HID,), dtype=jnp.float32)
        inp['mW2'] = jax.random.normal(ks[5], (D_HID, D_NODE), dtype=jnp.float32) / np.sqrt(D_HID)
        inp['mb2'] = jnp.zeros((D_NODE,), dtype=jnp.float32)
        d_in_upd = 2 * D_NODE
        inp['uW1'] = jax.random.normal(ks[6], (d_in_upd, D_HID), dtype=jnp.float32) / np.sqrt(d_in_upd)
        inp['ub1'] = jnp.zeros((D_HID,), dtype=jnp.float32)
        inp['uW2'] = jax.random.normal(ks[7], (D_HID, D_NODE), dtype=jnp.float32) / np.sqrt(D_HID)
        inp['ub2'] = jnp.zeros((D_NODE,), dtype=jnp.float32)
        return inp
    _L1_gnn_all = _L1_gnn_setup()
    _L1_gnn_in = {k: v for k, v in _L1_gnn_all.items() if k in ('mW1', 'mb1', 'mW2', 'mb2', 'uW1', 'ub1', 'uW2', 'ub2')}
    del _L1_gnn_all

    def _L2_gnn_setup():
        import jax, jax.numpy as jnp
        import numpy as np
        N, E = (12500, 200000)
        D_IN, D_HID, D_OUT = (64, 128, 64)
        BN_EPS = 1e-05
        L2_EPS = 1e-12

        def _xavier(key, shape):
            fan_in, fan_out = (shape[0], shape[1])
            a = np.sqrt(6.0 / (fan_in + fan_out)).astype(np.float32)
            return jax.random.uniform(key, shape, jnp.float32, -a, a)

        def _l2norm(h):
            n = jnp.sqrt(jnp.sum(h * h, axis=-1, keepdims=True))
            return h / jnp.maximum(n, L2_EPS)

        def _sage_mean(h, src, dst, Wl, Wr, b):
            msg = h[src]
            agg = jax.ops.segment_sum(msg, dst, num_segments=N)
            cnt = jax.ops.segment_sum(jnp.ones((src.shape[0], 1), h.dtype), dst, num_segments=N)
            mean = agg / jnp.maximum(cnt, 1.0)
            out = mean @ Wl + b + h @ Wr
            return _l2norm(out)
        key = jax.random.key(seed)
        ks = jax.random.split(key, 8)
        x = jax.random.normal(ks[0], (N, D_IN), jnp.float32)
        edge_index = jax.random.randint(ks[1], (2, E), 0, N)
        return dict(x=x, edge_index=edge_index, Wl1=_xavier(ks[2], (D_IN, D_HID)), Wr1=_xavier(ks[3], (D_IN, D_HID)), b1=jnp.zeros((D_HID,), jnp.float32), gamma1=jnp.ones((D_HID,), jnp.float32), beta1=jnp.zeros((D_HID,), jnp.float32), Wl2=_xavier(ks[4], (D_HID, D_OUT)), Wr2=_xavier(ks[5], (D_HID, D_OUT)), b2=jnp.zeros((D_OUT,), jnp.float32))
    _L2_gnn_all = _L2_gnn_setup()
    _L2_gnn_in = {k: v for k, v in _L2_gnn_all.items() if k in ('Wl1', 'Wr1', 'b1', 'gamma1', 'beta1', 'Wl2', 'Wr2', 'b2')}
    del _L2_gnn_all

    def _L3_gnn_setup():
        import jax, jax.numpy as jnp
        import numpy as np
        N_NODES = 6250
        N_EDGES = 100000
        D_IN = 64
        D_OUT = 64
        NUM_RELS = 16
        key = jax.random.key(seed)
        k1, k2, k3, k4, k5 = jax.random.split(key, 5)
        feat = jax.random.normal(k1, (N_NODES, D_IN), dtype=jnp.float32)
        weight = jax.random.normal(k2, (NUM_RELS, D_IN, D_OUT), dtype=jnp.float32) * 0.05
        src = jax.random.randint(k3, (N_EDGES,), 0, N_NODES, dtype=jnp.int32)
        dst = jax.random.randint(k4, (N_EDGES,), 0, N_NODES, dtype=jnp.int32)
        etypes = jax.random.randint(k5, (N_EDGES,), 0, NUM_RELS, dtype=jnp.int32)
        return {'feat': feat, 'weight': weight, 'src': src, 'dst': dst, 'etypes': etypes}
    _L3_gnn_all = _L3_gnn_setup()
    _L3_gnn_in = {k: v for k, v in _L3_gnn_all.items() if k in ('weight',)}
    del _L3_gnn_all
    return {'x': x, 'src': src, 'dst': dst, 'edge_attr_32': edge_attr_32, 'edge_type_16': edge_type_16, 'L0_gnn_W1': _L0_gnn_in['W1'], 'L0_gnn_b1': _L0_gnn_in['b1'], 'L0_gnn_W2': _L0_gnn_in['W2'], 'L0_gnn_b2': _L0_gnn_in['b2'], 'L1_gnn_mW1': _L1_gnn_in['mW1'], 'L1_gnn_mb1': _L1_gnn_in['mb1'], 'L1_gnn_mW2': _L1_gnn_in['mW2'], 'L1_gnn_mb2': _L1_gnn_in['mb2'], 'L1_gnn_uW1': _L1_gnn_in['uW1'], 'L1_gnn_ub1': _L1_gnn_in['ub1'], 'L1_gnn_uW2': _L1_gnn_in['uW2'], 'L1_gnn_ub2': _L1_gnn_in['ub2'], 'L2_gnn_Wl1': _L2_gnn_in['Wl1'], 'L2_gnn_Wr1': _L2_gnn_in['Wr1'], 'L2_gnn_b1': _L2_gnn_in['b1'], 'L2_gnn_gamma1': _L2_gnn_in['gamma1'], 'L2_gnn_beta1': _L2_gnn_in['beta1'], 'L2_gnn_Wl2': _L2_gnn_in['Wl2'], 'L2_gnn_Wr2': _L2_gnn_in['Wr2'], 'L2_gnn_b2': _L2_gnn_in['b2'], 'L3_gnn_weight': _L3_gnn_in['weight']}

def reference(x, src, dst, edge_attr_32, edge_type_16, L0_gnn_W1, L0_gnn_b1, L0_gnn_W2, L0_gnn_b2, L1_gnn_mW1, L1_gnn_mb1, L1_gnn_mW2, L1_gnn_mb2, L1_gnn_uW1, L1_gnn_ub1, L1_gnn_uW2, L1_gnn_ub2, L2_gnn_Wl1, L2_gnn_Wr1, L2_gnn_b1, L2_gnn_gamma1, L2_gnn_beta1, L2_gnn_Wl2, L2_gnn_Wr2, L2_gnn_b2, L3_gnn_weight):
    import jax
    import jax.numpy as jnp

    def _L0_gnn_ref(x, edge_index, W1, b1, W2, b2):
        import jax, jax.numpy as jnp
        import numpy as np
        N_NODES = 12500
        N_EDGES = 200000
        IN_DIM = 64
        HIDDEN = 256
        OUT_DIM = 64
        src, dst = (edge_index[0], edge_index[1])
        aggr = jax.ops.segment_sum(x[src], dst, num_segments=N_NODES)
        h = x + aggr
        h = jax.nn.elu(h @ W1 + b1)
        return h @ W2 + b2

    def _L1_gnn_ref(nodes, row, col, edge_features, mW1, mb1, mW2, mb2, uW1, ub1, uW2, ub2):
        import jax, jax.numpy as jnp
        import numpy as np
        N_NODES = 6250
        N_EDGES = 100000
        D_NODE = 64
        D_EDGE = 32
        D_HID = 128

        def _mlp(x, W1, b1, W2, b2):
            return jax.nn.relu(x @ W1 + b1) @ W2 + b2
        msg_in = jnp.concatenate([nodes[row], nodes[col], edge_features], axis=-1)
        messages = _mlp(msg_in, mW1, mb1, mW2, mb2)
        aggregated = jax.ops.segment_sum(messages, col, num_segments=nodes.shape[0])
        upd_in = jnp.concatenate([nodes, aggregated], axis=-1)
        return _mlp(upd_in, uW1, ub1, uW2, ub2)

    def _L2_gnn_ref(x, edge_index, Wl1, Wr1, b1, gamma1, beta1, Wl2, Wr2, b2):
        import jax, jax.numpy as jnp
        import numpy as np
        N, E = (12500, 200000)
        D_IN, D_HID, D_OUT = (64, 128, 64)
        BN_EPS = 1e-05
        L2_EPS = 1e-12

        def _xavier(key, shape):
            fan_in, fan_out = (shape[0], shape[1])
            a = np.sqrt(6.0 / (fan_in + fan_out)).astype(np.float32)
            return jax.random.uniform(key, shape, jnp.float32, -a, a)

        def _l2norm(h):
            n = jnp.sqrt(jnp.sum(h * h, axis=-1, keepdims=True))
            return h / jnp.maximum(n, L2_EPS)

        def _sage_mean(h, src, dst, Wl, Wr, b):
            msg = h[src]
            agg = jax.ops.segment_sum(msg, dst, num_segments=N)
            cnt = jax.ops.segment_sum(jnp.ones((src.shape[0], 1), h.dtype), dst, num_segments=N)
            mean = agg / jnp.maximum(cnt, 1.0)
            out = mean @ Wl + b + h @ Wr
            return _l2norm(out)
        src, dst = (edge_index[0], edge_index[1])
        h = _sage_mean(x, src, dst, Wl1, Wr1, b1)
        mu = jnp.mean(h, axis=0)
        var = jnp.mean((h - mu) ** 2, axis=0)
        h = gamma1 * (h - mu) * jax.lax.rsqrt(var + BN_EPS) + beta1
        h = jax.nn.relu(h)
        out = _sage_mean(h, src, dst, Wl2, Wr2, b2)
        out = out + x
        return _l2norm(out)

    def _L3_gnn_ref(feat, weight, src, dst, etypes):
        import jax, jax.numpy as jnp
        import numpy as np
        N_NODES = 6250
        N_EDGES = 100000
        D_IN = 64
        D_OUT = 64
        NUM_RELS = 16
        num_rels = weight.shape[0]
        h_src = feat[src]
        msg = jnp.zeros((h_src.shape[0], weight.shape[2]), dtype=feat.dtype)
        for r in range(num_rels):
            mask = etypes == r
            msg = msg + h_src * mask[:, None].astype(feat.dtype) @ weight[r]
        out = jax.ops.segment_sum(msg, dst, num_segments=feat.shape[0])
        return out
    edge_index = jnp.stack([src, dst])
    x = _layernorm(x + _L0_gnn_ref(x, edge_index, L0_gnn_W1, L0_gnn_b1, L0_gnn_W2, L0_gnn_b2), axis=-1)
    x = _layernorm(x + _L1_gnn_ref(x, src, dst, edge_attr_32, L1_gnn_mW1, L1_gnn_mb1, L1_gnn_mW2, L1_gnn_mb2, L1_gnn_uW1, L1_gnn_ub1, L1_gnn_uW2, L1_gnn_ub2), axis=-1)
    x = _layernorm(x + _L2_gnn_ref(x, edge_index, L2_gnn_Wl1, L2_gnn_Wr1, L2_gnn_b1, L2_gnn_gamma1, L2_gnn_beta1, L2_gnn_Wl2, L2_gnn_Wr2, L2_gnn_b2), axis=-1)
    x = _layernorm(x + _L3_gnn_ref(x, L3_gnn_weight, src, dst, edge_type_16), axis=-1)
    return x

_drawn_inputs = setup_inputs


def setup_inputs(seed=0):
    import zlib

    import numpy as np

    out = dict(_drawn_inputs(seed))
    spreads = {'L0_gnn_b1': (0.0, 0.362),
     'L0_gnn_b2': (0.0, 0.314),
     'L1_gnn_mb1': (0.0, 0.1),
     'L1_gnn_mb2': (0.0, 0.1),
     'L1_gnn_ub1': (0.0, 0.562),
     'L1_gnn_ub2': (0.0, 0.316),
     'L2_gnn_b1': (0.0, 0.8),
     'L2_gnn_gamma1': (1.0, 0.6),
     'L2_gnn_beta1': (0.0, 0.8),
     'L2_gnn_b2': (0.0, 0.8)}
    factors = {'L2_gnn_Wl1': 8.0, 'L2_gnn_Wr1': 7.363, 'L2_gnn_Wl2': 7.964, 'L2_gnn_Wr2': 5.671}
    for name, (base, spread) in spreads.items():
        noise = np.random.default_rng([zlib.crc32(name.encode()), seed]).standard_normal(out[name].shape)
        drawn = base * np.exp(spread * noise) if base else spread * noise
        out[name] = jnp.asarray(drawn.astype(out[name].dtype))
    for name, factor in factors.items():
        out[name] = (out[name] * factor).astype(out[name].dtype)
    return out
```

```python
from contextlib import ExitStack

import concourse.bass as bass
from concourse import mybir
from concourse.alu_op_type import AluOpType as ALU

F32 = mybir.dt.float32
I32 = mybir.dt.int32
BF16 = mybir.dt.bfloat16
ACT = mybir.ActivationFunctionType
AX = mybir.AxisListType

N = 12500
E = 200000
D = 64
H = 128
DE = 32
R = 16
P = 128
GROUP = 8
SUPER = GROUP * P
SLOTS = 4
SUPERS = -(-E // (SUPER * SLOTS)) * SLOTS
TURNS = SUPERS // SLOTS
CHUNKS = SUPERS * GROUP
UNIT = 250
HALF = UNIT // 2
UNITS = N // UNIT
NPAD = N + P + 44
LAYERS = 5
LN_EPS = 1e-5
BN_EPS = 1e-5
NORM_FLOOR_SQ = 1e-24
RMAX = bass.bass_isa.ReduceOp.max
SPANS_READY, TABLES_READY, PREP_READY = 8, 34, 36
ROWS_OUT = 6 * 16
CHAIN = [6, 4, 4, 12, 4]


def gnn_kernel(nc, x, xT, src_c, dst_c, dst_r, type_c, efT, W1, b1, W2, b2, mW1, mb1, mW2T, mb2,
               uW1, ub1, uW2, ub2, Wl1, Wr1, sb1, gamma, beta, Wl2, Wr2, sb2, Wrel, out):
    ctx = ExitStack()
    with ctx:
        def sb(name, shape, dt=F32):
            return ctx.enter_context(nc.sbuf_tensor(name, shape, dt))

        def sem(name):
            return ctx.enter_context(nc.semaphore(name))

        def dram(name, shape, dt=F32):
            return nc.dram_tensor(name, shape, dt, kind="Internal").ap()

        near_tab = dram("near_tab", [NPAD, H])
        far_tab = dram("far_tab", [N, H])
        x2_tab = dram("x2_tab", [N, D])
        h_tab = dram("h_tab", [N, D])
        rel_tab = dram("rel_tab", [N * R, D])
        dst_rows = dram("dst_rows", [2, (SUPERS + 1) * SUPER], BF16)

        X = sb("X", [P, 2 * UNITS, D + 1])
        AGG = sb("AGG", [P, NPAD])
        HT = sb("HT", [P, N])
        INV = sb("INV", [P, 2 * UNITS])
        SRC = sb("SRC", [P, CHUNKS + SLOTS * GROUP], I32)
        IDX3 = sb("IDX3", [P, CHUNKS + SLOTS * GROUP], I32)
        DREL = sb("DREL", [P, SUPERS, GROUP])
        FIRST = sb("FIRST", [P, SUPERS + 1])
        FIRSTP = sb("FIRSTP", [P, SUPERS + 1])
        FIRST_I = sb("FIRST_I", [1, SUPERS + 1], I32)
        WINS_I = sb("WINS_I", [1, SUPERS + 1], I32)
        FRONT_I = sb("FRONT_I", [1, TURNS + 1], I32)
        IDXB = sb("IDXB", [P, SLOTS, GROUP], I32)
        G = sb("G", [P, SLOTS, GROUP, P])
        OH = sb("OH", [P, 2, GROUP, P])
        DCUR = sb("DCUR", [P, GROUP])
        FCUR = sb("FCUR", [P, 1])
        TICK = sb("TICK", [1, SLOTS])
        EFT = HT[0:DE, 0:2 * SUPER].rearrange("p (b e) -> p b e", b=2)
        o = 2 * SUPER
        BW = HT[:, o:o + 2 * H].rearrange("p (b n) -> p b n", b=2)
        o += 2 * H
        BWX = HT[:, o:o + H]
        o += H
        OHT = HT[:, o:o + SUPER]
        o += SUPER
        HID = HT[:, o:o + SUPER]
        o += SUPER
        DROW = HT[0:2, o:o + SUPER].bitcast(BF16).rearrange("p (b e) -> p b e", b=2)
        o += SUPER
        DI = HT[:, o:o + CHUNKS].bitcast(I32)
        o += CHUNKS
        DF = HT[:, o:o + CHUNKS]
        o += CHUNKS
        T1 = HT[:, o:o + CHUNKS].bitcast(I32)
        o += CHUNKS
        HIB = OH[:, 0, 0:7, :].rearrange("p a b -> p (a b)")[:, 0:CHUNKS // 2].bitcast(BF16)
        LOB = OH[:, 1, 0:7, :].rearrange("p a b -> p (a b)")[:, 0:CHUNKS // 2].bitcast(BF16)
        FA = sb("FA", [1, 2, SUPERS])
        IOTA = sb("IOTA", [P, P])
        PIOTA = sb("PIOTA", [P, 1])
        IDENT = sb("IDENT", [P, P])
        ONES = sb("ONES", [P, HALF])
        ONES2 = sb("ONES2", [2, P], BF16)
        ZERO = sb("ZERO", [P, UNIT])
        w1 = sb("w1", [D, 2 * H])
        b1c = sb("b1c", [P, 2])
        w2 = sb("w2", [P, 2, D])
        rows = sb("rows", [1, 3 * D + 3 * H])
        b2r, ub2r, sb2r = rows[:, 0:D], rows[:, D:2 * D], rows[:, 2 * D:3 * D]
        mb1r = rows[:, 3 * D:3 * D + 2 * H]
        sb1r = rows[:, 3 * D + 2 * H:3 * D + 3 * H]
        wfn = sb("wfn", [D, 2 * H])
        wef = sb("wef", [DE, H])
        mw2T = sb("mw2T", [D, H])
        mb2c = sb("mb2c", [D, 1])
        uw1b = sb("uw1b", [D, H])
        u1 = sb("u1", [D + 1, H])
        mu = sb("mu", [H, H])
        ub1c = sb("ub1c", [P, 1])
        uw2 = sb("uw2", [P, D])
        wl1 = sb("wl1", [D, H])
        wr1 = sb("wr1", [D, H])
        gam = sb("gam", [P, 1])
        bet = sb("bet", [P, 1])
        wl2 = sb("wl2", [P, D])
        wr2 = sb("wr2", [P, D])
        wrel = sb("wrel", [D, R * D])
        Z = sb("Z", [P, UNIT])
        XU = sb("XU", [P, 2, D + 1])
        IU = sb("IU", [P, 2])
        XT = sb("XT", [D + 1, UNIT])
        POS = sb("POS", [P, 2 * UNIT])
        NEG = sb("NEG", [P, 2 * UNIT])
        HB = POS[:, :].rearrange("p (b n) -> p b n", b=2)
        Y = sb("Y", [P, 2, H])
        Y2 = sb("Y2", [P, 2, H])
        XS = sb("XS", [P, 2, D])
        ST6 = sb("ST6", [P, 2, 6])
        MV = sb("MV", [P, 2, 2])
        SS = sb("SS", [P, 2])
        VE = sb("VE", [P, 2])
        SQ = sb("SQ", [P, 2])
        RS = sb("RS", [P, 2])
        STG = sb("STG", [P, 2, R * D])
        MM = STG[:, 0, 0:2 * SUPERS]
        MR = STG[:, 1, 0:2 * SUPERS]
        BST = sb("BST", [P, UNITS, 6])
        BMV = sb("BMV", [P, 2])
        BT = sb("BT", [P, 4])
        BSC = sb("BSC", [P, 1])
        BSH = sb("BSH", [P, 1])

        def pb(name, shape):
            return ctx.enter_context(nc.psum_tensor(name, shape, F32))

        PBC = pb("PBC", [P, SUPER])
        PH = pb("PH", [P, SUPER])
        PAG = [pb("PAG0", [P, 512]), pb("PAG1", [P, 512])]
        NA = pb("NA", [P, 512])
        NB = pb("NB", [P, 512])
        PT = NB[:, 256:256 + UNIT]

        x_in = sem("x_in")
        loaded = sem("loaded")
        agg_zero = sem("agg_zero")
        zero_ready = sem("zero_ready")
        const_pool = sem("const_pool")
        prep = sem("prep")
        spans_out = sem("spans_out")
        rows_out = sem("rows_out")
        products = sem("products")
        idx_staged = [sem(f"idx_staged{h}") for h in range(SLOTS)]
        gathered = [sem(f"gathered{h}") for h in range(SLOTS)]
        released = sem("released")
        onehot_ready = sem("onehot_ready")
        summed = sem("summed")
        added = sem("added")
        pool_go, act_go, dve_go = sem("pool_go"), sem("act_go"), sem("dve_go")
        pe_go, sp_go = sem("pe_go"), sem("sp_go")
        far_hot = sem("far_hot")
        far_summed = sem("far_summed")
        far_step = sem("far_step")
        ef_in = [sem("ef_in0"), sem("ef_in1")]
        spread = sem("spread")
        hotT_ready = sem("hotT_ready")
        near_done = sem("near_done")
        pre_done = sem("pre_done")
        mixed = sem("mixed")
        relu_done = sem("relu_done")
        more_in = sem("more_in")
        more_hot = sem("more_hot")
        more_done = sem("more_done")
        staged = [sem(f"staged{p}") for p in range(LAYERS)]
        cleared = [sem(f"cleared{p}") for p in range(LAYERS)]
        chain = [sem(f"chain{p}") for p in range(LAYERS)]
        y_ready = [sem(f"y_ready{p}") for p in range(LAYERS)]
        var_ready = [sem(f"var_ready{p}") for p in range(LAYERS)]
        root_ready = [sem(f"root_ready{p}") for p in range(LAYERS)]
        x_new = [sem(f"x_new{p}") for p in range(LAYERS)]
        x_kept = [sem(f"x_kept{p}") for p in range(LAYERS)]
        flipped = [sem(f"flipped{p}") for p in range(LAYERS)]
        flip_copied = [sem(f"flip_copied{p}") for p in range(LAYERS)]
        stored = [sem(f"stored{p}") for p in range(LAYERS)]
        l0_hidden, l0_pos, l0_neg = sem("l0_hidden"), sem("l0_pos"), sem("l0_neg")
        l0_exp, l0_elu = sem("l0_exp"), sem("l0_elu")
        l0_maps, l0_maps_copied = sem("l0_maps"), sem("l0_maps_copied")
        l1_hidden, l1_relu = sem("l1_hidden"), sem("l1_relu")
        l2_products, l2_scaled, l2_normed = sem("l2_products"), sem("l2_scaled"), sem("l2_normed")
        l2_flipped, l2_kept, l2_stats = sem("l2_flipped"), sem("l2_kept"), sem("l2_stats")
        bn_step, bn_var, bn_root, bn_ready = sem("bn_step"), sem("bn_var"), sem("bn_root"), sem("bn_ready")
        bn_hot = sem("bn_hot")
        bn_map = sem("bn_map")
        bn_out = sem("bn_out")
        bn_stored = [sem("bn_stored0"), sem("bn_stored1")]
        l3_hot, l3_products, l3_scaled = sem("l3_hot"), sem("l3_products"), sem("l3_scaled")
        l3_map, l3_map_copied = sem("l3_map"), sem("l3_map_copied")

        early = [
            (SRC[:, 0:CHUNKS], src_c), (IDX3[:, 0:CHUNKS], type_c),
            (X[0:HALF, :, 0:D], x.rearrange("(a p) c -> p a c", p=HALF)),
            (w1[:, :], W1), (b1c[:, :], b1), (w2[:, :, :], W2.rearrange("(a p) c -> p a c", p=P)),
            (b2r, b2), (ub2r, ub2), (sb2r, sb2), (mb1r[:, H:2 * H], mb1), (sb1r, sb1),
            (wfn[:, 0:H], mW1[0:D, :]), (wfn[:, H:2 * H], mW1[D:2 * D, :]), (wef[:, :], mW1[2 * D:2 * D + DE, :]),
            (mw2T[:, :], mW2T), (mb2c[:, :], mb2), (u1[0:D, :], uW1[0:D, :]), (uw1b[:, :], uW1[D:2 * D, :]),
            (ub1c[:, :], ub1), (uw2[:, :], uW2), (wl1[:, :], Wl1), (wr1[:, :], Wr1), (gam[:, :], gamma),
            (bet[:, :], beta), (wl2[:, :], Wl2), (wr2[:, :], Wr2), (wrel[:, :], Wrel),
        ]
        ALL_LOADED = 16 * (len(early) + 1)

        block = ctx.enter_context(nc.Block())

        def rows_of(tab, u):
            return tab[bass.ds(u * UNIT, UNIT), :].rearrange("(a p) c -> p a c", p=HALF)

        def within(at):
            return nc.s_assert_within(at, 0, N)

        def node_units(eng, i, body):
            lo = eng.value_load(FRONT_I[0:1, bass.ds(i, 1)], min_val=0, max_val=UNITS)
            hi = eng.value_load(FRONT_I[0:1, bass.ds(i + 1, 1)], min_val=0, max_val=UNITS)
            with eng.If(hi > lo):
                with eng.Fori(lo, hi) as u:
                    body(nc.s_assert_within(u, 0, UNITS - 1))

        @block.sync
        def _(sp):
            sp.dma_start(DI, dst_c).then_inc(x_in, 16)
            sp.dma_start(T1, dst_r).then_inc(x_in, 16)
            for tile, array in early:
                sp.dma_start(tile, array).then_inc(loaded, 16)
            sp.wait_ge(agg_zero, 1)
            sp.dma_start(AGG[0:D, 0:N], xT).then_inc(loaded, 16)
            sp.wait_ge(zero_ready, 1)
            sp.dma_start(near_tab[N:N + P, :], ZERO[:, 0:H]).then_inc(rows_out, 16)
            sp.dma_start(near_tab[N + P:NPAD, :], ZERO[0:NPAD - N - P, 0:H]).then_inc(rows_out, 16)
            sp.wait_ge(prep, 4)
            for r, half in ((0, HIB), (1, LOB)):
                sp.dma_start(dst_rows[r, 0:SUPERS * SUPER].rearrange("(p c) -> p c", p=P), half).then_inc(rows_out, 16)
                sp.dma_start(dst_rows[r, SUPERS * SUPER:].rearrange("(p c) -> p c", p=P),
                             ZERO[:, 0:GROUP // 2].bitcast(BF16)).then_inc(rows_out, 16)

            sp.wait_ge(rows_out, ROWS_OUT)
            sp.wait_ge(prep, TABLES_READY)
            sp.wait_ge(stored[0], 32 * UNITS)

            def stream(s, b):
                w0 = sp.value_load(FIRST_I[0:1, bass.ds(s, 1)], min_val=0, max_val=N)
                sp.dma_start(EFT[:, b, :], efT[:, bass.ds(s * SUPER, SUPER)]).then_inc(ef_in[b], 16)
                sp.dma_start(DROW[:, b, :], dst_rows[:, bass.ds(s * SUPER, SUPER)]).then_inc(ef_in[b], 16)
                sp.dma_start(BW[:, b, :], near_tab[bass.ds(w0, P), :]).then_inc(ef_in[b], 16)
                n = sp.value_load(WINS_I[0:1, bass.ds(s, 1)], min_val=1, max_val=P)
                with sp.If(n > 1):
                    with sp.Fori(1, n) as it:
                        sp.reg_add(more, more, 1)
                        sp.wait_ge(more_done, sp.snap(more))
                        sp.dma_start(BWX, near_tab[bass.ds(within(w0 + it * P), P), :])\
                          .then_inc(more_in, 16)

            more = sp.alloc_register("sp_more")
            sp.reg_mov(more, 0)
            stream(0, 0)
            stream(1, 1)
            with sp.Fori(0, (SUPERS - 2) // 2) as i:
                for b in range(2):
                    sp.wait_ge(pre_done, 2 * i + b + 1)
                    sp.sem_inc(sp_go, 1)
                    stream(2 * i + b + 2, b)
            sp.wait_ge(pre_done, SUPERS - 1)
            stream(SUPERS, 0)
            with sp.Fori(0, UNITS // 2) as i:
                for b in range(2):
                    sp.wait_ge(bn_out, i * 2 + (b + 3))
                    sp.dma_start(rows_of(h_tab, i * 2 + b), STG[0:HALF, b, 0:2 * D].rearrange("p (a c) -> p a c", a=2))\
                      .then_inc(bn_stored[b], 16)
            sp.wait_ge(stored[4], 16 * UNITS)

        @block.gpsimd
        def _(pool):
            nc.gpsimd.iota(IOTA[:, :], [[1, P]], base=0, channel_multiplier=0,
                           allow_small_or_imprecise_dtypes=True).then_inc(const_pool, 1)
            nc.gpsimd.iota(PIOTA[:, :], [[0, 1]], base=0, channel_multiplier=1,
                           allow_small_or_imprecise_dtypes=True).then_inc(const_pool, 1)
            nc.gpsimd.memset(SRC[:, CHUNKS:], 0).then_inc(const_pool, 1)
            nc.gpsimd.memset(IDX3[:, CHUNKS:], 0).then_inc(const_pool, 1)
            pool.wait_ge(prep, SPANS_READY)
            nc.gpsimd.partition_all_reduce(MR, MM, P, RMAX).then_inc(spans_out, 1)
            tabs = [x, far_tab, x2_tab, h_tab, rel_tab]
            for p in range(LAYERS):
                if p == 0:
                    pool.wait_ge(const_pool, 4)
                if p == 1:
                    pool.wait_ge(stored[0], 32 * UNITS)
                if p == 2:
                    pool.wait_ge(stored[1], 16 * UNITS)
                if p == 3:
                    for b in range(2):
                        pool.wait_ge(bn_stored[b], 16 * (UNITS // 2))
                if p == 4:
                    pool.wait_ge(stored[3], 16 * UNITS)
                w = tabs[p].shape[1]
                with pool.Fori(0, TURNS) as i:
                    for h in range(SLOTS):
                        pool.wait_ge(idx_staged[h], i + ((TURNS + 1) * p + 1))
                        pool.wait_ge(released, i * SLOTS + (SUPERS * p + h + 1))
                        pool.sem_inc(pool_go, 1)
                        for j in range(GROUP):
                            pool.indirect_dma_start(
                                out=G[:, h, j, 0:w], out_offset=None, in_=tabs[p],
                                in_offset=bass.IndirectOffsetOnAxis(ap=IDXB[:, h, j:j + 1], axis=0),
                            ).then_inc(gathered[h], 16)

        @block.scalar
        def _(act):
            def root(p, u, n=1, k=0):
                act.wait_ge(var_ready[p], u * n + (k + 1))
                nc.scalar.activation(SQ[0:HALF, :], VE[0:HALF, :], ACT.Sqrt).then_inc(root_ready[p], 1)

            def flip_copy(p, u):
                m = D + 1 if p == 1 else D
                act.wait_ge(flipped[p], u + 1)
                nc.scalar.activation(XT[0:m, :], PT[0:m, :], ACT.Copy).then_inc(flip_copied[p], 1)

            def await_store(p, u, inc):
                act.wait_ge(stored[p], u * inc + inc)
                act.sem_inc(act_go, 1)

            def node0(u):
                act.wait_ge(l0_neg, u + 1)
                for a in range(2):
                    last = nc.scalar.activation(POS[:, a * UNIT:(a + 1) * UNIT], NA[:, a * UNIT:(a + 1) * UNIT],
                                                ACT.Relu, bias=b1c[:, a:a + 1])
                last.then_inc(l0_pos, 1)
                nc.scalar.activation(NEG[:, :], NEG[:, :], ACT.Exp).then_inc(l0_exp, 1)
                root(0, u)
                flip_copy(0, u)
                act.wait_ge(l0_maps, u + 1)
                nc.scalar.activation(STG[0:HALF, :, 0:2 * H], NA[0:HALF, :].rearrange("p (a c) -> p a c", a=2),
                                     ACT.Copy).then_inc(l0_maps_copied, 1)
                act.wait_ge(l0_maps_copied, u + 1)
                act.dma_start(rows_of(far_tab, u), STG[0:HALF, :, 0:H]).then_inc(stored[0], 16)
                act.dma_start(rows_of(near_tab, u), STG[0:HALF, :, H:2 * H]).then_inc(stored[0], 16)
                await_store(0, u, 32)

            def node1(u):
                flip_copy(1, u)
                act.wait_ge(l1_hidden, u + 1)
                nc.scalar.activation(POS[:, 0:UNIT], NA[:, 0:UNIT], ACT.Relu, bias=ub1c[:, 0:1]).then_inc(l1_relu, 1)
                root(1, u)
                act.wait_ge(x_new[1], u + 1)
                act.dma_start(rows_of(x2_tab, u), XS[0:HALF, :, :]).then_inc(stored[1], 16)
                await_store(1, u, 16)

            def node2(u):
                flip_copy(2, u)
                act.wait_ge(l2_products, u + 1)
                for a in range(2):
                    last = nc.scalar.activation(Y2[0:HALF, a, :], NA[0:HALF, a * H:(a + 1) * H], ACT.Copy,
                                                scale=IU[0:HALF, a:a + 1])
                last.then_inc(l2_scaled, 1)
                root(2, u)
                act.wait_ge(l2_flipped, u + 1)
                act.sem_inc(act_go, 1)
                nc.scalar.activation(HT[:, bass.ds(u * UNIT, UNIT)], NA[:, 0:UNIT], ACT.Copy).then_inc(l2_kept, 1)

            def normalized_hidden(u, b, ready):
                nc.scalar.activation(HB[:, b, :], HT[:, bass.ds(u * UNIT, UNIT)], ACT.Relu,
                                     bias=BSH[:, 0:1], scale=BSC[:, 0:1]).then_inc(ready, 1)

            def batch_norm_table():
                act.wait_ge(bn_var, 1)
                nc.scalar.activation(BT[:, 1:2], BT[:, 0:1], ACT.Sqrt).then_inc(bn_root, 1)
                act.wait_ge(bn_ready, 1)
                act.wait_ge(l2_kept, UNITS)
                act.sem_inc(act_go, 1)
                with act.Fori(0, UNITS // 2) as i:
                    for b in range(2):
                        act.wait_ge(bn_map, i * 2 + (b + 1))
                        act.sem_inc(act_go, 1)
                        normalized_hidden(i * 2 + b, b, bn_hot)

            def node3(u):
                normalized_hidden(u, 0, l3_hot)
                act.wait_ge(l3_products, u + 1)
                for a in range(2):
                    last = nc.scalar.activation(Y2[0:HALF, a, 0:D], NB[0:HALF, a * D:(a + 1) * D], ACT.Copy,
                                                scale=IU[0:HALF, a:a + 1])
                last.then_inc(l3_scaled, 1)
                for k in range(3):
                    root(3, u, 3, k)
                flip_copy(3, u)
                for k in range(4):
                    act.wait_ge(l3_map, u * 4 + (k + 1))
                    nc.scalar.activation(STG[0:HALF, k // 2, (k % 2) * 512:(k % 2) * 512 + 512],
                                         (NA, NB)[k % 2][0:HALF, :], ACT.Copy).then_inc(l3_map_copied, 1)
                act.wait_ge(l3_map_copied, u * 4 + 4)
                act.dma_start(rows_of(rel_tab.rearrange("(n r) d -> n (r d)", r=R), u), STG[0:HALF, :, :])\
                   .then_inc(stored[3], 16)
                await_store(3, u, 16)

            def node4(u):
                root(4, u)
                act.wait_ge(x_new[4], u + 1)
                act.dma_start(rows_of(out, u), XS[0:HALF, :, :]).then_inc(stored[4], 16)
                await_store(4, u, 16)

            node = [node0, node1, node2, node3, node4]
            act.wait_ge(const_pool, 4)
            act.wait_ge(loaded, ALL_LOADED)
            act.wait_ge(prep, TABLES_READY)
            act.sem_inc(act_go, 1)
            for p in range(LAYERS):
                numbers = IDX3 if p == 4 else SRC
                for h in range(SLOTS):
                    if p:
                        act.wait_ge(gathered[h], 16 * GROUP * TURNS * p)
                    nc.scalar.copy(IDXB[:, h, :], numbers[:, h * GROUP:(h + 1) * GROUP]).then_inc(idx_staged[h], 1)
                with act.Fori(0, TURNS) as i:
                    for h in range(SLOTS):
                        if p == 1:
                            act.wait_ge(mixed, i * SLOTS + (h + 1))
                            nc.scalar.activation(HID, HID, ACT.Relu).then_inc(relu_done, 1)
                        act.wait_ge(gathered[h], i * (16 * GROUP) + 16 * GROUP * (TURNS * p + 1))
                        act.sem_inc(act_go, 1)
                        nc.scalar.copy(IDXB[:, h, :], numbers[:, bass.ds(i * (SLOTS * GROUP) + (SLOTS + h) * GROUP, GROUP)])\
                          .then_inc(idx_staged[h], 1)
                    node_units(act, i, node[p])
                if p == 2:
                    batch_norm_table()

        @block.vector
        def _(dve):
            step = [0]

            def link(ins):
                step[0] += 1
                ins.then_inc(prep, 1)
                dve.wait_ge(prep, step[0])

            nc.vector.memset(ZERO[:, :], 0.0).then_inc(zero_ready, 1)
            nc.vector.memset(AGG[:, :], 0.0).then_inc(agg_zero, 1)
            nc.vector.memset(ONES[:, :], 1.0)
            nc.vector.memset(ONES2[:, :], 1.0)
            nc.vector.memset(rows[:, 3 * D:3 * D + H], 0.0)
            nc.vector.memset(G[:, :, :, D:P], 1.0).then_inc(released, 1)
            dve.sem_inc(released, SLOTS - 1)
            dve.wait_ge(x_in, 32)
            HALVES = DF.bitcast(I32)
            link(nc.vector.tensor_single_scalar(HALVES, T1, -P, ALU.bitwise_and))
            link(nc.vector.tensor_copy(HIB, HALVES))
            link(nc.vector.tensor_single_scalar(HALVES, T1, P - 1, ALU.bitwise_and))
            link(nc.vector.tensor_copy(LOB, HALVES))
            link(nc.vector.tensor_copy(DF, DI))
            DFv = DF.rearrange("p (s j) -> p s j", j=GROUP)
            link(nc.vector.tensor_reduce(MM[:, 0:SUPERS], DFv, AX.X, ALU.max))
            link(nc.vector.tensor_reduce(MR[:, 0:SUPERS], DFv, AX.X, ALU.min))
            link(nc.vector.tensor_scalar_mul(MM[:, SUPERS:], MR[:, 0:SUPERS], -1.0))
            assert step[0] == SPANS_READY
            dve.wait_ge(spans_out, 1)
            link(nc.vector.memset(FIRST[:, SUPERS:], 0.0))
            link(nc.vector.memset(WINS_I[:, SUPERS:], 1))
            link(nc.vector.tensor_scalar_mul(FIRST[:, 0:SUPERS], MR[:, SUPERS:], -1.0))
            dve.wait_ge(const_pool, 2)
            link(nc.vector.tensor_scalar(FIRSTP[:, :], FIRST[:, :], PIOTA[:, 0:1], None, ALU.add))
            link(nc.vector.tensor_copy(FIRST_I[:, :], FIRST[0:1, :]))
            link(nc.vector.tensor_tensor(DREL[:, :, :], DFv,
                                         FIRST[:, 0:SUPERS].unsqueeze(2).to_broadcast([P, SUPERS, GROUP]),
                                         ALU.subtract))
            link(nc.vector.tensor_tensor(FA[:, 0, 0:SUPERS], MR[0:1, 0:SUPERS], FIRST[0:1, 0:SUPERS], ALU.subtract))
            link(nc.vector.tensor_copy(WINS_I[:, 0:SUPERS], FA[:, 0, 0:SUPERS]))
            link(nc.vector.tensor_single_scalar(WINS_I[:, 0:SUPERS], WINS_I[:, 0:SUPERS], 7, ALU.logical_shift_right))
            link(nc.vector.tensor_scalar(WINS_I[:, 0:SUPERS], WINS_I[:, 0:SUPERS], 1.0, None, ALU.add))
            link(nc.vector.memset(FA[:, :, :], float(N)))
            link(nc.vector.tensor_reduce(FA[:, 0, 0:TURNS], FIRST[0:1, 0:SUPERS].rearrange("p (i h) -> p i h", h=SLOTS),
                                         AX.X, ALU.min))
            a = 0
            for k in (1, 2, 4, 8, 16, 32):
                link(nc.vector.tensor_tensor(FA[:, 1 - a, 0:TURNS], FA[:, a, 0:TURNS], FA[:, a, k:k + TURNS], ALU.min))
                a = 1 - a
            link(nc.vector.tensor_scalar(FA[:, 1 - a, 0:TURNS], FA[:, a, 0:TURNS], -(UNIT - 1) / 2, 1.0 / UNIT,
                                         ALU.add, ALU.mult))
            link(nc.vector.tensor_scalar_max(FA[:, a, 0:TURNS], FA[:, 1 - a, 0:TURNS], 0.0))
            link(nc.vector.tensor_copy(FRONT_I[:, 0:TURNS], FA[:, a, 0:TURNS]))
            link(nc.vector.memset(FRONT_I[:, 0:1], 0))
            link(nc.vector.memset(FRONT_I[:, TURNS:], UNITS))
            dve.wait_ge(loaded, ALL_LOADED)
            link(nc.vector.tensor_scalar(DI, SRC[:, 0:CHUNKS], float(R), None, ALU.mult))
            link(nc.vector.tensor_tensor(IDX3[:, 0:CHUNKS], IDX3[:, 0:CHUNKS], DI, ALU.add))
            link(nc.vector.tensor_scalar(IDENT[:, :], IOTA[:, :], PIOTA[:, 0:1], None, ALU.is_equal))
            assert step[0] == TABLES_READY
            dve.wait_ge(products, 1)
            link(nc.vector.tensor_copy(mu[:, :], NA[:, 0:H]))
            link(nc.vector.tensor_copy(u1[D:D + 1, :], NB[0:1, 0:H]))
            dve.wait_ge(rows_out, ROWS_OUT)
            dve.sem_inc(added, 1)
            assert step[0] == PREP_READY, step[0]

            far = dve.alloc_register("dve_far")
            steps = dve.alloc_register("dve_steps")
            more = dve.alloc_register("dve_more")
            for reg in (far, steps, more):
                dve.reg_mov(reg, 0)

            def far_link(ins):
                ins.then_inc(far_step, 1)
                dve.reg_add(steps, steps, 1)
                dve.wait_ge(far_step, dve.snap(steps))
                dve.sem_inc(dve_go, 1)

            def one_hot(b, d):
                return nc.vector.tensor_tensor(OH[:, b, :, :], IOTA[:, :].unsqueeze(1).to_broadcast([P, GROUP, P]),
                                               d.unsqueeze(2).to_broadcast([P, GROUP, P]), ALU.is_equal)

            def targets(s):
                return DREL[:, bass.ds(s, 1), :].rearrange("p a j -> p (a j)")

            def add_window(b, m, at):
                dst = AGG[0:m, bass.ds(at, P)]
                return nc.vector.tensor_tensor(dst, dst, PAG[b][0:m, 0:P], ALU.add)

            def add_super(p, i, h, w0, n, m):
                b = h % 2
                dve.wait_ge(summed, i * SLOTS + (SUPERS * p + h + 1))
                dve.wait_ge(added, i * SLOTS + (SUPERS * p + h + 1))
                add_window(b, m, w0).then_inc(added, 1)
                with dve.If(n > 1):
                    dve.wait_ge(added, i * SLOTS + (SUPERS * p + h + 2))
                    far_link(nc.vector.tensor_scalar(DCUR[:, :], targets(i * SLOTS + h), 0.0, None, ALU.add))
                    with dve.Fori(1, n) as it:
                        far_link(nc.vector.tensor_scalar(DCUR[:, :], DCUR[:, :], -float(P), None, ALU.add))
                        one_hot(b, DCUR[:, :]).then_inc(far_hot, 1)
                        dve.reg_add(far, far, 1)
                        dve.wait_ge(far_summed, dve.snap(far))
                        far_link(add_window(b, m, within(w0 + it * P)))

            def release(h):
                nc.vector.memset(TICK[:, h:h + 1], 0.0).then_inc(released, 1)

            def hot_T(t, first=False):
                dve.wait_ge(spread, t + 1)
                if not first:
                    dve.wait_ge(pre_done, t)
                nc.vector.tensor_scalar(OHT, PBC[:, :], FIRSTP[:, bass.ds(t, 1)], None, ALU.is_equal)\
                  .then_inc(hotT_ready, 1)

            def more_hot_T(t):
                n = dve.value_load(WINS_I[0:1, bass.ds(t, 1)], min_val=1, max_val=P)
                with dve.If(n > 1):
                    dve.wait_ge(near_done, t + 1)
                    far_link(nc.vector.tensor_scalar(FCUR[:, :], FIRSTP[:, bass.ds(t, 1)], 0.0, None, ALU.add))
                    with dve.Fori(1, n) as it:
                        far_link(nc.vector.tensor_scalar(FCUR[:, :], FCUR[:, :], float(P), None, ALU.add))
                        dve.reg_add(more, more, 1)
                        dve.wait_ge(more_done, dve.snap(more))
                        nc.vector.tensor_scalar(OHT, PBC[:, :], FCUR[:, 0:1], None, ALU.is_equal).then_inc(more_hot, 1)

            def move(dst, src_):
                return nc.vector.tensor_scalar(dst, src_, 1.0, None, ALU.mult)

            def steps_of(p, u):
                count = [0]

                def run(*instructions):
                    count[0] += 1
                    instructions[-1].then_inc(chain[p], 1)
                    dve.wait_ge(chain[p], u * CHAIN[p] + count[0])

                def done():
                    assert count[0] == CHAIN[p], (p, count[0])
                return run, done

            def fetch(p, u, m):
                move(Z[0:m, :], AGG[0:m, bass.ds(u * UNIT, UNIT)])
                if p in (2, 3):
                    move(IU[0:HALF, :], INV[0:HALF, bass.ds(u * 2, 2)])
                last = move(XU[0:HALF, :, :] if p else XU[0:HALF, :, 0:D],
                            X[0:HALF, bass.ds(u * 2, 2), :] if p else X[0:HALF, bass.ds(u * 2, 2), 0:D])
                last.then_inc(staged[p], 1)
                dve.wait_ge(staged[p], u + 1)
                nc.vector.tensor_scalar(AGG[:, bass.ds(u * UNIT, UNIT)], ZERO[:, :], 0.0, None, ALU.add)\
                  .then_inc(cleared[p], 1)

            def layer_norm(p, u, run, n=1, k=0):
                run(nc.vector.bn_stats(ST6[0:HALF, 0, :], Y[0:HALF, 0, 0:D]),
                    nc.vector.bn_stats(ST6[0:HALF, 1, :], Y[0:HALF, 1, 0:D]))
                dve.sem_inc(dve_go, 1)
                run(nc.vector.bn_aggr(MV[0:HALF, 0, :], ST6[0:HALF, 0, :]),
                    nc.vector.bn_aggr(MV[0:HALF, 1, :], ST6[0:HALF, 1, :]))
                nc.vector.tensor_scalar(VE[0:HALF, :], MV[0:HALF, :, 1], LN_EPS, None, ALU.add).then_inc(var_ready[p], 1)
                dve.wait_ge(root_ready[p], u * n + (k + 1))
                run(nc.vector.reciprocal(RS[0:HALF, :], SQ[0:HALF, :]))
                for a_ in range(2):
                    last = nc.vector.tensor_scalar(XS[0:HALF, a_, :], Y[0:HALF, a_, 0:D], MV[0:HALF, a_, 0:1],
                                                   RS[0:HALF, a_:a_ + 1], ALU.subtract, ALU.mult)
                last.then_inc(x_new[p], 1)
                if p < 4:
                    dve.wait_ge(x_new[p], u + 1)
                    move(X[0:HALF, bass.ds(u * 2, 2), 0:D], XS[0:HALF, :, :]).then_inc(x_kept[p], 1)

            def inverse_norm(p, u, run, w, n, k):
                y = Y[0:HALF, :, 0:w]
                run(nc.vector.tensor_tensor(Y2[0:HALF, :, 0:w], y, y, ALU.mult))
                run(nc.vector.tensor_reduce(SS[0:HALF, :], Y2[0:HALF, :, 0:w], AX.X, ALU.add))
                nc.vector.tensor_scalar(VE[0:HALF, :], SS[0:HALF, :], NORM_FLOOR_SQ, None, ALU.max)\
                  .then_inc(var_ready[p], 1)
                dve.wait_ge(root_ready[p], u * n + (k + 1))
                run(nc.vector.reciprocal(RS[0:HALF, :], SQ[0:HALF, :]))

            def halves(t, w=D):
                return t.rearrange("p (a c) -> p a c", c=w)

            def node0(u):
                run, done = steps_of(0, u)
                fetch(0, u, D + 1)
                dve.wait_ge(l0_hidden, u + 1)
                for a_ in range(2):
                    last = nc.vector.tensor_scalar(NEG[:, a_ * UNIT:(a_ + 1) * UNIT], NA[:, a_ * UNIT:(a_ + 1) * UNIT],
                                                   b1c[:, a_:a_ + 1], 0.0, ALU.add, ALU.min)
                last.then_inc(l0_neg, 1)
                degree = NB[0:HALF, 508:510]
                move(X[0:HALF, bass.ds(u * 2, 2), D], degree)
                run(nc.vector.tensor_scalar(IU[0:HALF, :], degree, 1.0, None, ALU.max))
                run(nc.vector.reciprocal(SS[0:HALF, :], IU[0:HALF, :]))
                move(INV[0:HALF, bass.ds(u * 2, 2)], SS[0:HALF, :])
                dve.wait_ge(l0_pos, u + 1)
                dve.wait_ge(l0_exp, u + 1)
                nc.vector.scalar_tensor_tensor(NEG[:, :], NEG[:, :], -1.0, POS[:, :], ALU.add, ALU.add).then_inc(l0_elu, 1)
                dve.wait_ge(y_ready[0], u + 1)
                run(nc.vector.tensor_tensor(Y[0:HALF, :, 0:D], halves(NB[0:HALF, 0:2 * D]), XU[0:HALF, :, 0:D], ALU.add))
                layer_norm(0, u, run)
                done()

            def node1(u):
                run, done = steps_of(1, u)
                fetch(1, u, H)
                dve.wait_ge(y_ready[1], u + 1)
                run(nc.vector.tensor_tensor(Y[0:HALF, :, 0:D], halves(NB[0:HALF, 0:2 * D]), XU[0:HALF, :, 0:D], ALU.add))
                layer_norm(1, u, run)
                done()

            def node2(u):
                run, done = steps_of(2, u)
                fetch(2, u, D)
                dve.wait_ge(l2_scaled, u + 1)
                run(nc.vector.tensor_tensor(Y[0:HALF, :, :], halves(NB[0:HALF, 0:2 * H], H), Y2[0:HALF, :, :], ALU.add))
                inverse_norm(2, u, run, H, 1, 0)
                for a_ in range(2):
                    last = nc.vector.tensor_scalar(Y2[0:HALF, a_, :], Y[0:HALF, a_, :], RS[0:HALF, a_:a_ + 1], None, ALU.mult)
                last.then_inc(l2_normed, 1)
                dve.wait_ge(l2_kept, u + 1)
                dve.sem_inc(dve_go, 1)
                nc.vector.bn_stats(BST[:, bass.ds(u, 1), :].rearrange("p a c -> p (a c)"), NA[:, 0:UNIT]).then_inc(l2_stats, 1)
                done()

            def batch_norm_table():
                dve.wait_ge(l2_stats, UNITS)
                nc.vector.bn_aggr(BMV[:, :], BST[:, :, :].rearrange("p u c -> p (u c)")).then_inc(bn_step, 1)
                dve.wait_ge(bn_step, 1)
                nc.vector.tensor_scalar(BT[:, 0:1], BMV[:, 1:2], BN_EPS, None, ALU.add).then_inc(bn_var, 1)
                dve.wait_ge(bn_root, 1)
                nc.vector.reciprocal(BT[:, 2:3], BT[:, 1:2]).then_inc(bn_step, 1)
                dve.wait_ge(bn_step, 2)
                nc.vector.tensor_tensor(BSC[:, :], BT[:, 2:3], gam[:, :], ALU.mult).then_inc(bn_step, 1)
                dve.wait_ge(bn_step, 3)
                nc.vector.tensor_tensor(BT[:, 3:4], BMV[:, 0:1], BSC[:, :], ALU.mult).then_inc(bn_step, 1)
                dve.wait_ge(bn_step, 4)
                nc.vector.tensor_tensor(BSH[:, :], bet[:, :], BT[:, 3:4], ALU.subtract).then_inc(bn_ready, 1)

                def rows_out_of_psum(u, b, first):
                    dve.wait_ge(bn_map, u + 3)
                    if not first:
                        dve.wait_ge(bn_stored[b], (u - b) * 8)
                    move(STG[0:HALF, b, 0:2 * D], (NA, NB)[b][0:HALF, 0:2 * D]).then_inc(bn_out, 1)

                for b in range(2):
                    rows_out_of_psum(b, b, True)
                with dve.Fori(1, UNITS // 2) as i:
                    for b in range(2):
                        rows_out_of_psum(i * 2 + b, b, False)

            def node3(u):
                run, done = steps_of(3, u)
                fetch(3, u, D)
                dve.wait_ge(l3_scaled, u + 1)
                run(nc.vector.tensor_tensor(Y[0:HALF, :, 0:D], halves(NA[0:HALF, 0:2 * D]), Y2[0:HALF, :, 0:D], ALU.add))
                for k in range(2):
                    inverse_norm(3, u, run, D, 3, k)
                    run(*[nc.vector.scalar_tensor_tensor(Y[0:HALF, a_, 0:D], Y[0:HALF, a_, 0:D], RS[0:HALF, a_:a_ + 1],
                                                         XU[0:HALF, a_, 0:D], ALU.mult, ALU.add) for a_ in range(2)])
                layer_norm(3, u, run, 3, 2)
                done()

            def node4(u):
                run, done = steps_of(4, u)
                fetch(4, u, D)
                dve.wait_ge(y_ready[4], u + 1)
                run(nc.vector.tensor_tensor(Y[0:HALF, :, 0:D], halves(NB[0:HALF, 0:2 * D]), XU[0:HALF, :, 0:D], ALU.add))
                layer_norm(4, u, run)
                done()

            node = [node0, node1, node2, node3, node4]
            for p in range(LAYERS):
                m = (D + 1, H, D, D, D)[p]
                if p:
                    dve.wait_ge(cleared[p - 1], UNITS)
                    if p != 3:
                        dve.wait_ge(x_kept[p - 1], UNITS)
                    dve.sem_inc(dve_go, 1)
                if p == 1:
                    hot_T(0, first=True)
                    more_hot_T(0)
                with dve.Fori(0, TURNS) as i:
                    for h in range(SLOTS):
                        s = i * SLOTS + h
                        w0 = dve.value_load(FIRST_I[0:1, bass.ds(s, 1)], min_val=0, max_val=N)
                        n = dve.value_load(WINS_I[0:1, bass.ds(s, 1)], min_val=1, max_val=P)
                        one_hot(h % 2, targets(s)).then_inc(onehot_ready, 1)
                        if p == 1:
                            hot_T(s + 1)
                            dve.wait_ge(pre_done, i * SLOTS + (h + 1))
                            dve.wait_ge(gathered[h], i * (16 * GROUP) + 16 * GROUP * (TURNS * p + 1))
                            nc.vector.tensor_tensor(HID, PH[:, :], G[:, h, :, :].rearrange("p j c -> p (j c)"), ALU.add)\
                              .then_inc(mixed, 1)
                            release(h)
                            more_hot_T(s + 1)
                        add_super(p, i, h, w0, n, m)
                        if p != 1:
                            release(h)
                    dve.wait_ge(added, i * SLOTS + (SUPERS * p + SLOTS + 1))
                    dve.sem_inc(dve_go, 1)
                    node_units(dve, i, node[p])
                if p == 2:
                    batch_norm_table()

        @block.tensor
        def _(pe):
            def mm(dst, lhsT, rhs, start=True, stop=True):
                return nc.tensor.matmul(dst, lhsT, rhs, start=start, stop=stop, skip_group_check=True)

            def with_bias(dst, lhsT, rhs, bias):
                mm(dst, lhsT, rhs, stop=False)
                return mm(dst, ONES[0:1, 0:HALF], bias, start=False)

            def half(a):
                return slice(a * HALF, (a + 1) * HALF)

            pe.sem_inc(more_done, 1)
            pe.sem_inc(bn_map, 2)
            pe.sem_inc(bn_out, 2)
            pe.wait_ge(loaded, ALL_LOADED)
            mm(NA[:, 0:H], mw2T[:, :], uw1b[:, :])
            mm(NB[0:1, 0:H], mb2c[:, :], uw1b[:, :]).then_inc(products, 1)
            pe.wait_ge(prep, PREP_READY)
            pe.sem_inc(pe_go, 1)
            far = pe.alloc_register("pe_far")
            more = pe.alloc_register("pe_more")
            for reg in (far, more):
                pe.reg_mov(reg, 0)

            def sum_window(p, h, m):
                msg = HID.rearrange("p (j c) -> p j c", j=GROUP) if p == 1 else G[:, h, :, :]
                for j in range(GROUP):
                    last = mm(PAG[h % 2][0:m, 0:P], msg[:, j, 0:m], OH[:, h % 2, j, :], j == 0, j == GROUP - 1)
                return last

            def sum_super(p, i, h, n, m):
                pe.wait_ge(onehot_ready, i * SLOTS + (SUPERS * p + h + 1))
                if p == 1:
                    pe.wait_ge(relu_done, i * SLOTS + (h + 1))
                else:
                    pe.wait_ge(gathered[h], i * (16 * GROUP) + 16 * GROUP * (TURNS * p + 1))
                sum_window(p, h, m).then_inc(summed, 1)
                with pe.If(n > 1):
                    with pe.Fori(1, n) as it:
                        pe.reg_add(far, far, 1)
                        pe.wait_ge(far_hot, pe.snap(far))
                        sum_window(p, h, m).then_inc(far_summed, 1)

            def pre(t, b, uses, first=False):
                n = pe.value_load(WINS_I[0:1, bass.ds(t, 1)], min_val=1, max_val=P)
                pe.wait_ge(ef_in[b], uses * 48)
                pe.sem_inc(pe_go, 1)
                for q in range(2):
                    last = mm(PBC[:, q * 512:(q + 1) * 512], ONES2[:, :], DROW[:, b, q * 512:(q + 1) * 512])
                last.then_inc(spread, 1)
                pe.wait_ge(hotT_ready, t + 1)
                if not first:
                    pe.wait_ge(mixed, t)
                for j in range(GROUP):
                    c = slice(j * P, (j + 1) * P)
                    last = mm(PH[:, c], OHT[:, c], BW[:, b, :], j % 4 == 0, False)
                last.then_inc(near_done, 1)
                with pe.If(n > 1):
                    with pe.Fori(1, n) as it:
                        pe.reg_add(more, more, 1)
                        window = pe.snap(more)
                        landed = pe.snap(window * 16)
                        pe.wait_ge(more_in, landed)
                        pe.wait_ge(more_hot, window)
                        for j in range(GROUP):
                            c = slice(j * P, (j + 1) * P)
                            last = mm(PH[:, c], OHT[:, c], BWX, False, False)
                        last.then_inc(more_done, 1)
                for j in range(GROUP):
                    c = slice(j * P, (j + 1) * P)
                    last = mm(PH[:, c], EFT[:, b, c], wef[:, :], False, j % 4 == 3)
                last.then_inc(pre_done, 1)

            def flip(p, tile, m):
                for a in range(2):
                    last = mm(PT[0:m, half(a)], tile[0:HALF, a, 0:m], IDENT[0:HALF, 0:HALF])
                last.then_inc(flipped[p], 1)

            def node0(u):
                pe.wait_ge(staged[0], u + 1)
                for a in range(2):
                    mm(NA[:, a * UNIT:(a + 1) * UNIT], w1[:, a * H:(a + 1) * H], Z[0:D, :])
                    last = mm(NB[0:HALF, 508 + a:509 + a], Z[D:D + 1, half(a)], ONES[D:D + 1, 0:1])
                last.then_inc(l0_hidden, 1)
                pe.wait_ge(l0_elu, u + 1)
                for a in range(2):
                    dst = NB[0:HALF, a * D:(a + 1) * D]
                    mm(dst, NEG[:, half(a)], w2[:, 0, :], stop=False)
                    mm(dst, NEG[:, UNIT + a * HALF:UNIT + (a + 1) * HALF], w2[:, 1, :], False, False)
                    last = mm(dst, ONES[0:1, 0:HALF], b2r, False)
                last.then_inc(y_ready[0], 1)
                pe.wait_ge(x_new[0], u + 1)
                flip(0, XS, D)
                pe.wait_ge(flip_copied[0], u + 1)
                for a in range(2):
                    last = with_bias(NA[0:HALF, a * 2 * H:(a + 1) * 2 * H], XT[0:D, half(a)], wfn[:, :], mb1r)
                last.then_inc(l0_maps, 1)
                pe.wait_ge(l0_maps_copied, u + 1)
                pe.sem_inc(pe_go, 1)

            def node1(u):
                pe.wait_ge(staged[1], u + 1)
                flip(1, XU, D + 1)
                pe.wait_ge(flip_copied[1], u + 1)
                mm(NA[:, 0:UNIT], u1[:, :], XT[:, :], stop=False)
                mm(NA[:, 0:UNIT], mu[:, :], Z[:, :], False).then_inc(l1_hidden, 1)
                pe.wait_ge(l1_relu, u + 1)
                for a in range(2):
                    last = with_bias(NB[0:HALF, a * D:(a + 1) * D], POS[:, half(a)], uw2[:, :], ub2r)
                last.then_inc(y_ready[1], 1)

            def node2(u):
                pe.wait_ge(staged[2], u + 1)
                flip(2, XU, D)
                pe.wait_ge(flip_copied[2], u + 1)
                for a in range(2):
                    mm(NA[0:HALF, a * H:(a + 1) * H], Z[0:D, half(a)], wl1[:, :])
                    last = with_bias(NB[0:HALF, a * H:(a + 1) * H], XT[0:D, half(a)], wr1[:, :], sb1r)
                last.then_inc(l2_products, 1)
                pe.wait_ge(l2_normed, u + 1)
                for a in range(2):
                    last = mm(NA[:, half(a)], Y2[0:HALF, a, :], IDENT[0:HALF, 0:HALF])
                last.then_inc(l2_flipped, 1)

            def batch_norm_table():
                with pe.Fori(0, UNITS // 2) as i:
                    for b in range(2):
                        pe.wait_ge(bn_hot, i * 2 + (b + 1))
                        pe.wait_ge(bn_out, i * 2 + (b + 1))
                        for a in range(2):
                            last = mm((NA, NB)[b][0:HALF, a * D:(a + 1) * D], HB[:, b, half(a)], wl2[:, :])
                        last.then_inc(bn_map, 1)

            def node3(u):
                pe.wait_ge(staged[3], u + 1)
                pe.wait_ge(l3_hot, u + 1)
                for a in range(2):
                    mm(NB[0:HALF, a * D:(a + 1) * D], Z[0:D, half(a)], IDENT[0:D, 0:D])
                    last = with_bias(NA[0:HALF, a * D:(a + 1) * D], HB[:, 0, half(a)], wr2[:, :], sb2r)
                last.then_inc(l3_products, 1)
                pe.wait_ge(x_new[3], u + 1)
                flip(3, XS, D)
                pe.wait_ge(flip_copied[3], u + 1)
                for k in range(4):
                    if k >= 2:
                        pe.wait_ge(l3_map_copied, u * 4 + (k - 1))
                    mm((NA, NB)[k % 2][0:HALF, :], XT[0:D, half(k // 2)], wrel[:, (k % 2) * 512:(k % 2) * 512 + 512])\
                        .then_inc(l3_map, 1)

            def node4(u):
                pe.wait_ge(staged[4], u + 1)
                for a in range(2):
                    last = mm(NB[0:HALF, a * D:(a + 1) * D], Z[0:D, half(a)], IDENT[0:D, 0:D])
                last.then_inc(y_ready[4], 1)

            node = [node0, node1, node2, node3, node4]
            for p in range(LAYERS):
                m = (D + 1, H, D, D, D)[p]
                if p == 1:
                    pre(0, 0, 1, first=True)
                with pe.Fori(0, TURNS) as i:
                    for h in range(SLOTS):
                        n = pe.value_load(WINS_I[0:1, bass.ds(i * SLOTS + h, 1)], min_val=1, max_val=P)
                        if p == 1:
                            pre(i * SLOTS + (h + 1), (h + 1) % 2, i * (SLOTS // 2) + ((h + 1) // 2 + 1))
                        sum_super(p, i, h, n, m)
                    node_units(pe, i, node[p])
                if p == 2:
                    batch_norm_table()


def kernel(x, src, dst, edge_attr_32, edge_type_16, L0_gnn_W1, L0_gnn_b1, L0_gnn_W2, L0_gnn_b2,
           L1_gnn_mW1, L1_gnn_mb1, L1_gnn_mW2, L1_gnn_mb2, L1_gnn_uW1, L1_gnn_ub1, L1_gnn_uW2, L1_gnn_ub2,
           L2_gnn_Wl1, L2_gnn_Wr1, L2_gnn_b1, L2_gnn_gamma1, L2_gnn_beta1, L2_gnn_Wl2, L2_gnn_Wr2, L2_gnn_b2,
           L3_gnn_weight):
    import numpy as np
    import concourse.bacc as bacc
    from concourse.bass_utils import run_bass_kernel_spmd

    def padded(a, last, fill):
        a = np.asarray(a)
        out = np.full(a.shape[:-1] + (last,), fill, a.dtype)
        out[..., :a.shape[-1]] = a
        return out

    def by_chunk(a, fill):
        return padded(a, CHUNKS * P, fill).reshape(CHUNKS, P).T

    def column(a):
        return np.asarray(a).reshape(-1, 1)

    def row(a):
        return np.asarray(a).reshape(1, -1)

    arrays = {
        "x": x, "xT": np.asarray(x).T,
        "src_c": by_chunk(src, 0), "dst_c": by_chunk(dst, N), "dst_r": padded(dst, CHUNKS * P, N).reshape(P, CHUNKS),
        "type_c": by_chunk(edge_type_16, 0), "efT": padded(np.asarray(edge_attr_32).T, (SUPERS + 1) * SUPER, 0),
        "W1": L0_gnn_W1, "b1": np.asarray(L0_gnn_b1).reshape(2, P).T, "W2": L0_gnn_W2, "b2": row(L0_gnn_b2),
        "mW1": L1_gnn_mW1, "mb1": row(L1_gnn_mb1), "mW2T": np.asarray(L1_gnn_mW2).T, "mb2": column(L1_gnn_mb2),
        "uW1": L1_gnn_uW1, "ub1": column(L1_gnn_ub1), "uW2": L1_gnn_uW2, "ub2": row(L1_gnn_ub2),
        "Wl1": L2_gnn_Wl1, "Wr1": L2_gnn_Wr1, "sb1": row(L2_gnn_b1), "gamma": column(L2_gnn_gamma1),
        "beta": column(L2_gnn_beta1), "Wl2": L2_gnn_Wl2, "Wr2": L2_gnn_Wr2, "sb2": row(L2_gnn_b2),
        "Wrel": np.asarray(L3_gnn_weight).transpose(1, 0, 2).reshape(D, R * D),
    }
    arrays = {name: np.ascontiguousarray(a) for name, a in arrays.items()}
    nc = bacc.Bacc("TRN2", target_bir_lowering=False, num_devices=1)
    args = [nc.dram_tensor(f"in_{name}", a.shape, mybir.dt.from_np(a.dtype), kind="ExternalInput").ap()
            for name, a in arrays.items()]
    out = nc.dram_tensor("out", (N, D), F32, kind="ExternalOutput").ap()
    gnn_kernel(nc, *args, out)
    r = run_bass_kernel_spmd(nc, [{f"in_{name}": a for name, a in arrays.items()}], core_ids=[0])
    return r.results[0]["out"]
```

```python
from contextlib import ExitStack

import concourse.bass as bass
from concourse import mybir
from concourse.alu_op_type import AluOpType as ALU

F32 = mybir.dt.float32
I32 = mybir.dt.int32
I16 = mybir.dt.int16
ACT = mybir.ActivationFunctionType
AX = mybir.AxisListType

N = 12500
E = 200000
D = 64
H = 128
DE = 32
R = 16
P = 128
GROUP = 8
SUPER = GROUP * P
SLOTS = 4
SUPERS = -(-E // (SUPER * SLOTS)) * SLOTS
TURNS = SUPERS // SLOTS
CHUNKS = SUPERS * GROUP
UNIT = 250
HALF = UNIT // 2
UNITS = N // UNIT
WIN = P - DE
NPAD = N + P + 44
LAYERS = 5
LN_EPS = 1e-5
BN_EPS = 1e-5
NORM_FLOOR_SQ = 1e-24
RMAX = bass.bass_isa.ReduceOp.max
SPANS_READY, TABLES_READY, PREP_READY = 6, 43, 45
ROWS_OUT = 4 * 16
CHAIN = [6, 4, 4, 12, 4]


def gnn_kernel(nc, x, xT, src_c, dst_c, dst_r, type_c, efT, W1, b1, W2, b2, mW1, mb1, mW2T, mb2,
               uW1, ub1, uW2, ub2, Wl1, Wr1, sb1, gamma, beta, Wl2, Wr2, sb2, Wrel, out):
    ctx = ExitStack()
    with ctx:
        def sb(name, shape, dt=F32):
            return ctx.enter_context(nc.sbuf_tensor(name, shape, dt))

        def sem(name):
            return ctx.enter_context(nc.semaphore(name))

        def dram(name, shape, dt=F32):
            return nc.dram_tensor(name, shape, dt, kind="Internal").ap()

        near_tab = dram("near_tab", [NPAD, H])
        far_tab = dram("far_tab", [N, H])
        x2_tab = dram("x2_tab", [N, D])
        h_tab = dram("h_tab", [N, D])
        rel_tab = dram("rel_tab", [N * R, D])
        dst_rows = dram("dst_rows", [1, (SUPERS + 2) * SUPER], I16)

        X = sb("X", [P, 2 * UNITS, D + 1])
        AGG = sb("AGG", [P, NPAD])
        HT = sb("HT", [P, N])
        INV = sb("INV", [P, 2 * UNITS])
        SRC = sb("SRC", [P, CHUNKS + SLOTS * GROUP], I32)
        IDX3 = sb("IDX3", [P, CHUNKS + SLOTS * GROUP], I32)
        DREL = sb("DREL", [P, SUPERS + 1, GROUP])
        FIRST = sb("FIRST", [P, SUPERS + 2])
        FIRSTP = sb("FIRSTP", [P, SUPERS + 2])
        FIRST_I = sb("FIRST_I", [1, SUPERS + 2], I32)
        WINS_I = sb("WINS_I", [1, SUPERS + 2], I32)
        DONE_I = sb("DONE_I", [1, TURNS + 1], I32)
        FRONT_I = sb("FRONT_I", [1, TURNS], I32)
        IDXB = sb("IDXB", [P, SLOTS, GROUP], I32)
        G = sb("G", [P, SLOTS, GROUP, P])
        OH = sb("OH", [P, 2, GROUP, WIN])
        DCUR = sb("DCUR", [P, GROUP])
        FCUR = sb("FCUR", [P, 1])
        TICK = sb("TICK", [1, SLOTS])
        MIXT = HT[:, 0:2 * SUPER].rearrange("p (b e) -> p b e", b=2)
        o = 2 * SUPER
        MIXW = HT[:, o:o + 2 * H].rearrange("p (b n) -> p b n", b=2)
        o += 2 * H
        MOREW = HT[0:WIN, o:o + H]
        o += H
        HID = HT[:, o:o + 2 * SUPER].rearrange("p (b e) -> p b e", b=2)
        o += 2 * SUPER
        DROW = HT[0:WIN, o:o + SUPER].bitcast(I16).rearrange("p (b e) -> p b e", b=2)
        o += SUPER
        DI = HT[:, o:o + CHUNKS].bitcast(I32)
        o += CHUNKS
        DF = HT[:, o:o + CHUNKS]
        o += CHUNKS
        T1 = HT[:, o:o + CHUNKS].bitcast(I32)
        o += CHUNKS
        DST16 = HT[:, o:o + CHUNKS // 2].bitcast(I16)
        FA = sb("FA", [1, 2, SUPERS])
        IOTA = sb("IOTA", [P, P])
        PIOTA = sb("PIOTA", [P, 1])
        IDENT = sb("IDENT", [P, P])
        ONES = sb("ONES", [P, HALF])
        ZERO = sb("ZERO", [P, UNIT])
        w1 = sb("w1", [D, 2 * H])
        b1c = sb("b1c", [P, 2])
        w2 = sb("w2", [P, 2, D])
        rows = sb("rows", [1, 3 * D + 3 * H])
        b2r, ub2r, sb2r = rows[:, 0:D], rows[:, D:2 * D], rows[:, 2 * D:3 * D]
        mb1r = rows[:, 3 * D:3 * D + 2 * H]
        sb1r = rows[:, 3 * D + 2 * H:3 * D + 3 * H]
        wfn = sb("wfn", [D, 2 * H])
        mw2T = sb("mw2T", [D, H])
        mb2c = sb("mb2c", [D, 1])
        uw1b = sb("uw1b", [D, H])
        u1 = sb("u1", [D + 1, H])
        mu = sb("mu", [H, H])
        ub1c = sb("ub1c", [P, 1])
        uw2 = sb("uw2", [P, D])
        wl1 = sb("wl1", [D, H])
        wr1 = sb("wr1", [D, H])
        gam = sb("gam", [P, 1])
        bet = sb("bet", [P, 1])
        wl2 = sb("wl2", [P, D])
        wr2 = sb("wr2", [P, D])
        wrel = sb("wrel", [D, R * D])
        Z = sb("Z", [P, UNIT])
        XU = sb("XU", [P, 2, D + 1])
        IU = sb("IU", [P, 2])
        XT = sb("XT", [D + 1, UNIT])
        POS = sb("POS", [P, 2 * UNIT])
        NEG = sb("NEG", [P, 2 * UNIT])
        HB = POS[:, :].rearrange("p (b n) -> p b n", b=2)
        Y = sb("Y", [P, 2, H])
        Y2 = sb("Y2", [P, 2, H])
        XS = sb("XS", [P, 2, D])
        ST6 = sb("ST6", [P, 2, 6])
        MV = sb("MV", [P, 2, 2])
        SS = sb("SS", [P, 2])
        VE = sb("VE", [P, 2])
        SQ = sb("SQ", [P, 2])
        RS = sb("RS", [P, 2])
        STG = sb("STG", [P, 2, R * D])
        MM = STG[:, 0, 0:2 * SUPERS]
        MR = STG[:, 1, 0:2 * SUPERS]
        BST = sb("BST", [P, UNITS, 6])
        BMV = sb("BMV", [P, 2])
        BT = sb("BT", [P, 4])
        BSC = sb("BSC", [P, 1])
        BSH = sb("BSH", [P, 1])

        def pb(name, shape):
            return ctx.enter_context(nc.psum_tensor(name, shape, F32))

        PH = [pb("PH0", [P, SUPER]), pb("PH1", [P, SUPER])]
        PAG = [pb("PAG0", [P, 512]), pb("PAG1", [P, 512])]
        NA = pb("NA", [P, 512])
        NB = pb("NB", [P, 512])
        PT = NB[:, 256:256 + UNIT]

        x_in = sem("x_in")
        src_in = sem("src_in")
        loaded = sem("loaded")
        agg_zero = sem("agg_zero")
        zero_ready = sem("zero_ready")
        const_pool = sem("const_pool")
        prep = sem("prep")
        spans_out = sem("spans_out")
        rows_out = sem("rows_out")
        products = sem("products")
        idx_staged = [sem(f"idx_staged{h}") for h in range(SLOTS)]
        gathered = [sem(f"gathered{h}") for h in range(SLOTS)]
        released = sem("released")
        onehot_ready = sem("onehot_ready")
        summed = sem("summed")
        added = sem("added")
        pool_go, act_go, dve_go = sem("pool_go"), sem("act_go"), sem("dve_go")
        pe_go, sp_go = sem("pe_go"), sem("sp_go")
        far_hot = sem("far_hot")
        far_summed = sem("far_summed")
        far_step = sem("far_step")
        ef_in = [sem("ef_in0"), sem("ef_in1")]
        hotT_ready = sem("hotT_ready")
        pre_done = sem("pre_done")
        mixed = sem("mixed")
        relu_done = sem("relu_done")
        more_in = sem("more_in")
        more_hot = sem("more_hot")
        more_done = sem("more_done")
        staged = [sem(f"staged{p}") for p in range(LAYERS)]
        cleared = [sem(f"cleared{p}") for p in range(LAYERS)]
        chain = [sem(f"chain{p}") for p in range(LAYERS)]
        y_ready = [sem(f"y_ready{p}") for p in range(LAYERS)]
        var_ready = [sem(f"var_ready{p}") for p in range(LAYERS)]
        root_ready = [sem(f"root_ready{p}") for p in range(LAYERS)]
        x_new = [sem(f"x_new{p}") for p in range(LAYERS)]
        x_kept = [sem(f"x_kept{p}") for p in range(LAYERS)]
        flipped = [sem(f"flipped{p}") for p in range(LAYERS)]
        flip_copied = [sem(f"flip_copied{p}") for p in range(LAYERS)]
        stored = [sem(f"stored{p}") for p in range(LAYERS)]
        l0_hidden, l0_pos, l0_neg = sem("l0_hidden"), sem("l0_pos"), sem("l0_neg")
        l0_exp, l0_elu = sem("l0_exp"), sem("l0_elu")
        l0_maps, l0_maps_copied = sem("l0_maps"), sem("l0_maps_copied")
        l1_hidden, l1_relu = sem("l1_hidden"), sem("l1_relu")
        l2_products, l2_scaled, l2_normed = sem("l2_products"), sem("l2_scaled"), sem("l2_normed")
        l2_flipped, l2_kept, l2_stats = sem("l2_flipped"), sem("l2_kept"), sem("l2_stats")
        bn_step, bn_var, bn_root, bn_ready = sem("bn_step"), sem("bn_var"), sem("bn_root"), sem("bn_ready")
        bn_hot = sem("bn_hot")
        bn_map = sem("bn_map")
        bn_out = sem("bn_out")
        bn_stored = [sem("bn_stored0"), sem("bn_stored1")]
        l3_hot, l3_products, l3_scaled = sem("l3_hot"), sem("l3_products"), sem("l3_scaled")
        l3_map, l3_map_copied = sem("l3_map"), sem("l3_map_copied")

        early = [
            (IDX3[:, 0:CHUNKS], type_c),
            (X[0:HALF, :, 0:D], x.rearrange("(a p) c -> p a c", p=HALF)),
            (w1[:, :], W1), (b1c[:, :], b1), (w2[:, :, :], W2.rearrange("(a p) c -> p a c", p=P)),
            (b2r, b2), (ub2r, ub2), (sb2r, sb2), (mb1r[:, H:2 * H], mb1), (sb1r, sb1),
            (wfn[:, 0:H], mW1[0:D, :]), (wfn[:, H:2 * H], mW1[D:2 * D, :]), 
            (MIXW[WIN:P, 0, :], mW1[2 * D:2 * D + DE, :]), (MIXW[WIN:P, 1, :], mW1[2 * D:2 * D + DE, :]),
            (mw2T[:, :], mW2T), (mb2c[:, :], mb2), (u1[0:D, :], uW1[0:D, :]), (uw1b[:, :], uW1[D:2 * D, :]),
            (ub1c[:, :], ub1), (uw2[:, :], uW2), (wl1[:, :], Wl1), (wr1[:, :], Wr1), (gam[:, :], gamma),
            (bet[:, :], beta), (wl2[:, :], Wl2), (wr2[:, :], Wr2), (wrel[:, :], Wrel),
        ]
        ALL_LOADED = 16 * (len(early) + 1)

        block = ctx.enter_context(nc.Block())

        def rows_of(tab, u):
            return tab[bass.ds(u * UNIT, UNIT), :].rearrange("(a p) c -> p a c", p=HALF)

        def within(at):
            return nc.s_assert_within(at, 0, N)

        def unit_of_turn(eng, i):
            return [eng.value_load(DONE_I[0:1, bass.ds(i + k, 1)], min_val=0, max_val=UNITS) for k in range(2)]

        def stage_of_turn(eng, turn_units, node, h):
            lo, hi = turn_units
            with eng.If(hi > lo):
                node(nc.s_assert_within(lo, 0, UNITS - 1), h)

        def last_units(eng, node):
            lo = eng.value_load(DONE_I[0:1, TURNS:TURNS + 1], min_val=0, max_val=UNITS)
            with eng.Fori(lo, UNITS) as u:
                for h in range(SLOTS):
                    node(nc.s_assert_within(u, 0, UNITS - 1), h)

        STORE = [32, 16, 0, 16, 16]

        def all_stored(p):
            return STORE[p] * (UNITS + 1)

        def slot_gathered(p, i):
            return i * (16 * GROUP) + 16 * GROUP * (TURNS * p + 1)

        @block.sync
        def _(sp):
            sp.dma_start(SRC[:, 0:CHUNKS], src_c).then_inc(src_in, 16)
            sp.dma_start(DI, dst_c).then_inc(x_in, 16)
            sp.dma_start(T1, dst_r).then_inc(x_in, 16)
            for tile, array in early:
                sp.dma_start(tile, array).then_inc(loaded, 16)
            sp.wait_ge(agg_zero, 1)
            sp.dma_start(AGG[0:D, 0:N], xT).then_inc(loaded, 16)
            sp.wait_ge(zero_ready, 1)
            sp.dma_start(near_tab[N:N + P, :], ZERO[:, 0:H]).then_inc(rows_out, 16)
            sp.dma_start(near_tab[N + P:NPAD, :], ZERO[0:NPAD - N - P, 0:H]).then_inc(rows_out, 16)
            sp.wait_ge(prep, 1)
            sp.dma_start(dst_rows[0, 0:SUPERS * SUPER].rearrange("(p c) -> p c", p=P), DST16).then_inc(rows_out, 16)
            sp.dma_start(dst_rows[0, SUPERS * SUPER:].rearrange("(p c) -> p c", p=P),
                         ZERO[:, 0:GROUP].bitcast(I16)).then_inc(rows_out, 16)

            def stream(s, b):
                w0 = sp.value_load(FIRST_I[0:1, bass.ds(s, 1)], min_val=0, max_val=N)
                sp.dma_start(MIXT[WIN:P, b, :], efT[:, bass.ds(s * SUPER, SUPER)]).then_inc(ef_in[b], 16)
                sp.dma_start(DROW[:, b, :], dst_rows[:, bass.ds(s * SUPER, SUPER)].to_broadcast([WIN, SUPER]))\
                  .then_inc(ef_in[b], 16)
                sp.dma_start(MIXW[0:WIN, b, :], near_tab[bass.ds(w0, WIN), :]).then_inc(ef_in[b], 16)
                n = sp.value_load(WINS_I[0:1, bass.ds(s, 1)], min_val=1, max_val=P + 4)
                with sp.If(n > 1):
                    with sp.Fori(1, n) as it:
                        sp.reg_add(more, more, 1)
                        sp.wait_ge(more_done, sp.snap(more))
                        sp.dma_start(MOREW, near_tab[bass.ds(within(w0 + it * WIN), WIN), :])\
                          .then_inc(more_in, 16)
                    sp.wait_ge(more_done, sp.snap(sp.snap(more) + 1))
                    sp.sem_inc(sp_go, 1)

            more = sp.alloc_register("sp_more")
            sp.reg_mov(more, 0)
            for p in range(LAYERS):
                numbers = IDX3 if p == 4 else SRC
                if p == 0:
                    sp.wait_ge(const_pool, 4)
                    sp.wait_ge(src_in, 16)
                if p == 4:
                    sp.wait_ge(prep, TABLES_READY)
                for h in range(SLOTS):
                    if p:
                        sp.wait_ge(gathered[h], 16 * GROUP * TURNS * p)
                        sp.wait_ge(idx_staged[h], 16 * (TURNS + 1) * p)
                    sp.dma_start(IDXB[:, h, :], numbers[:, h * GROUP:(h + 1) * GROUP]).then_inc(idx_staged[h], 16)
                if p == 1:
                    sp.wait_ge(rows_out, ROWS_OUT)
                    sp.wait_ge(prep, TABLES_READY)
                    sp.wait_ge(stored[0], all_stored(0))
                    stream(0, 0)
                    stream(1, 1)
                with sp.Fori(0, TURNS) as i:
                    for h in range(SLOTS):
                        sp.wait_ge(gathered[h], slot_gathered(p, i))
                        sp.sem_inc(sp_go, 1)
                        sp.dma_start(IDXB[:, h, :], numbers[:, bass.ds(i * (SLOTS * GROUP) + (SLOTS + h) * GROUP, GROUP)])\
                          .then_inc(idx_staged[h], 16)
                        if p == 1:
                            sp.wait_ge(pre_done, i * SLOTS + (h + 2))
                            sp.sem_inc(sp_go, 1)
                            stream(i * SLOTS + (h + 2), h % 2)
                if p == 2:
                    with sp.Fori(0, UNITS // 2) as i:
                        for b in range(2):
                            sp.wait_ge(bn_out, i * 2 + (b + 3))
                            sp.dma_start(rows_of(h_tab, i * 2 + b),
                                         STG[0:HALF, b, 0:2 * D].rearrange("p (a c) -> p a c", a=2))\
                              .then_inc(bn_stored[b], 16)
            for h in range(SLOTS):
                sp.wait_ge(idx_staged[h], 16 * (TURNS + 1) * LAYERS)
            sp.wait_ge(stored[4], all_stored(4))

        @block.gpsimd
        def _(pool):
            nc.gpsimd.iota(IOTA[:, :], [[1, P]], base=0, channel_multiplier=0,
                           allow_small_or_imprecise_dtypes=True).then_inc(const_pool, 1)
            nc.gpsimd.iota(PIOTA[:, :], [[0, 1]], base=0, channel_multiplier=1,
                           allow_small_or_imprecise_dtypes=True).then_inc(const_pool, 1)
            nc.gpsimd.memset(SRC[:, CHUNKS:], 0).then_inc(const_pool, 1)
            nc.gpsimd.memset(IDX3[:, CHUNKS:], 0).then_inc(const_pool, 1)
            pool.wait_ge(prep, SPANS_READY)
            nc.gpsimd.partition_all_reduce(MR, MM, P, RMAX).then_inc(spans_out, 1)
            tabs = [x, far_tab, x2_tab, h_tab, rel_tab]
            for p in range(LAYERS):
                if p == 0:
                    pool.wait_ge(const_pool, 4)
                if p == 1:
                    pool.wait_ge(stored[0], all_stored(0))
                if p == 2:
                    pool.wait_ge(stored[1], all_stored(1))
                if p == 3:
                    for b in range(2):
                        pool.wait_ge(bn_stored[b], 16 * (UNITS // 2))
                if p == 4:
                    pool.wait_ge(stored[3], all_stored(3))
                w = tabs[p].shape[1]
                with pool.Fori(0, TURNS) as i:
                    for h in range(SLOTS):
                        pool.wait_ge(idx_staged[h], i * 16 + 16 * ((TURNS + 1) * p + 1))
                        pool.wait_ge(released, i * SLOTS + (SUPERS * p + h + 1))
                        pool.sem_inc(pool_go, 1)
                        for j in range(GROUP):
                            pool.indirect_dma_start(
                                out=G[:, h, j, 0:w], out_offset=None, in_=tabs[p],
                                in_offset=bass.IndirectOffsetOnAxis(ap=IDXB[:, h, j:j + 1], axis=0),
                            ).then_inc(gathered[h], 16)

        @block.scalar
        def _(act):
            def root(p, u, n=1, k=0):
                act.wait_ge(var_ready[p], u * n + (k + 1))
                nc.scalar.activation(SQ[0:HALF, :], VE[0:HALF, :], ACT.Sqrt).then_inc(root_ready[p], 1)

            def flip_copy(p, u):
                m = D + 1 if p == 1 else D
                act.wait_ge(flipped[p], u + 1)
                nc.scalar.activation(XT[0:m, :], PT[0:m, :], ACT.Copy).then_inc(flip_copied[p], 1)

            def tile_free(p, u):
                act.wait_ge(stored[p], u * STORE[p] + STORE[p])
                act.sem_inc(act_go, 1)

            def node0(u, stage):
                if stage == 1:
                    act.wait_ge(l0_neg, u + 1)
                    for a in range(2):
                        last = nc.scalar.activation(POS[:, a * UNIT:(a + 1) * UNIT], NA[:, a * UNIT:(a + 1) * UNIT],
                                                    ACT.Relu, bias=b1c[:, a:a + 1])
                    last.then_inc(l0_pos, 1)
                    nc.scalar.activation(NEG[:, :], NEG[:, :], ACT.Exp).then_inc(l0_exp, 1)
                if stage == 2:
                    root(0, u)
                if stage == 3:
                    flip_copy(0, u)
                    tile_free(0, u)
                    act.wait_ge(l0_maps, u + 1)
                    nc.scalar.activation(STG[0:HALF, :, 0:2 * H], NA[0:HALF, :].rearrange("p (a c) -> p a c", a=2),
                                         ACT.Copy).then_inc(l0_maps_copied, 1)
                    act.wait_ge(l0_maps_copied, u + 1)
                    act.dma_start(rows_of(far_tab, u), STG[0:HALF, :, 0:H]).then_inc(stored[0], 16)
                    act.dma_start(rows_of(near_tab, u), STG[0:HALF, :, H:2 * H]).then_inc(stored[0], 16)

            def node1(u, stage):
                if stage == 1:
                    flip_copy(1, u)
                if stage == 2:
                    act.wait_ge(l1_hidden, u + 1)
                    nc.scalar.activation(POS[:, 0:UNIT], NA[:, 0:UNIT], ACT.Relu, bias=ub1c[:, 0:1])\
                        .then_inc(l1_relu, 1)
                if stage == 3:
                    root(1, u)
                    act.wait_ge(x_new[1], u + 1)
                    act.dma_start(rows_of(x2_tab, u), XS[0:HALF, :, :]).then_inc(stored[1], 16)

            def node2(u, stage):
                if stage == 1:
                    flip_copy(2, u)
                if stage == 2:
                    act.wait_ge(l2_products, u + 1)
                    for a in range(2):
                        last = nc.scalar.activation(Y2[0:HALF, a, :], NA[0:HALF, a * H:(a + 1) * H], ACT.Copy,
                                                    scale=IU[0:HALF, a:a + 1])
                    last.then_inc(l2_scaled, 1)
                    root(2, u)
                if stage == 3:
                    act.wait_ge(l2_flipped, u + 1)
                    act.sem_inc(act_go, 1)
                    nc.scalar.activation(HT[:, bass.ds(u * UNIT, UNIT)], NA[:, 0:UNIT], ACT.Copy).then_inc(l2_kept, 1)

            def normalized_hidden(u, b, ready):
                nc.scalar.activation(HB[:, b, :], HT[:, bass.ds(u * UNIT, UNIT)], ACT.Relu,
                                     bias=BSH[:, 0:1], scale=BSC[:, 0:1]).then_inc(ready, 1)

            def batch_norm_table():
                act.wait_ge(bn_var, 1)
                nc.scalar.activation(BT[:, 1:2], BT[:, 0:1], ACT.Sqrt).then_inc(bn_root, 1)
                act.wait_ge(bn_ready, 1)
                act.wait_ge(l2_kept, UNITS)
                act.sem_inc(act_go, 1)
                with act.Fori(0, UNITS // 2) as i:
                    for b in range(2):
                        act.wait_ge(bn_map, i * 2 + (b + 1))
                        act.sem_inc(act_go, 1)
                        normalized_hidden(i * 2 + b, b, bn_hot)

            def node3(u, stage):
                if stage == 0:
                    normalized_hidden(u, 0, l3_hot)
                if stage == 1:
                    act.wait_ge(l3_products, u + 1)
                    for a in range(2):
                        last = nc.scalar.activation(Y2[0:HALF, a, 0:D], NB[0:HALF, a * D:(a + 1) * D], ACT.Copy,
                                                    scale=IU[0:HALF, a:a + 1])
                    last.then_inc(l3_scaled, 1)
                if stage == 2:
                    for k in range(3):
                        root(3, u, 3, k)
                if stage == 3:
                    flip_copy(3, u)
                    tile_free(3, u)
                    for k in range(4):
                        act.wait_ge(l3_map, u * 4 + (k + 1))
                        nc.scalar.activation(STG[0:HALF, k // 2, (k % 2) * 512:(k % 2) * 512 + 512],
                                             (NA, NB)[k % 2][0:HALF, :], ACT.Copy).then_inc(l3_map_copied, 1)
                    act.wait_ge(l3_map_copied, u * 4 + 4)
                    act.dma_start(rows_of(rel_tab.rearrange("(n r) d -> n (r d)", r=R), u), STG[0:HALF, :, :])\
                       .then_inc(stored[3], 16)

            def node4(u, stage):
                if stage == 2:
                    root(4, u)
                if stage == 3:
                    act.wait_ge(x_new[4], u + 1)
                    act.dma_start(rows_of(out, u), XS[0:HALF, :, :]).then_inc(stored[4], 16)

            node = [node0, node1, node2, node3, node4]
            for p in range(LAYERS):
                if STORE[p]:
                    act.sem_inc(stored[p], STORE[p])
            act.wait_ge(loaded, ALL_LOADED)
            act.wait_ge(prep, TABLES_READY)
            act.sem_inc(act_go, 1)
            for p in range(LAYERS):
                if p == 2:
                    act.wait_ge(ef_in[1], 48 * (SUPERS // 2 + 1))
                if p == 3:
                    act.wait_ge(bn_map, UNITS + 2)
                with act.Fori(0, TURNS) as i:
                    turn_units = unit_of_turn(act, i)
                    for h in range(SLOTS):
                        if p == 1:
                            act.wait_ge(mixed, i * SLOTS + (h + 2))
                            nc.scalar.activation(HID[:, h % 2, :], HID[:, h % 2, :], ACT.Relu).then_inc(relu_done, 1)
                        stage_of_turn(act, turn_units, node[p], h)
                last_units(act, node[p])
                if p == 2:
                    batch_norm_table()

        @block.vector
        def _(dve):
            step = [0]

            def link(ins):
                step[0] += 1
                ins.then_inc(prep, 1)
                dve.wait_ge(prep, step[0])

            nc.vector.memset(ZERO[:, :], 0.0).then_inc(zero_ready, 1)
            nc.vector.memset(AGG[:, :], 0.0).then_inc(agg_zero, 1)
            nc.vector.memset(ONES[:, :], 1.0)
            nc.vector.memset(rows[:, 3 * D:3 * D + H], 0.0)
            nc.vector.memset(G[:, :, :, D:P], 1.0).then_inc(released, 1)
            dve.sem_inc(released, SLOTS - 1)
            dve.wait_ge(x_in, 32)
            link(nc.vector.tensor_copy(DST16, T1))
            link(nc.vector.tensor_copy(DF, DI))
            DFv = DF.rearrange("p (s j) -> p s j", j=GROUP)
            link(nc.vector.tensor_reduce(MM[:, 0:SUPERS], DFv, AX.X, ALU.max))
            link(nc.vector.tensor_reduce(MR[:, 0:SUPERS], DFv, AX.X, ALU.min))
            link(nc.vector.tensor_scalar_mul(MM[:, SUPERS:], MR[:, 0:SUPERS], -1.0))
            link(nc.vector.memset(FIRST[:, SUPERS:], 0.0))
            assert step[0] == SPANS_READY
            dve.wait_ge(spans_out, 1)
            link(nc.vector.memset(WINS_I[:, SUPERS:], 1))
            link(nc.vector.tensor_scalar_mul(FIRST[:, 0:SUPERS], MR[:, SUPERS:], -1.0))
            dve.wait_ge(const_pool, 2)
            link(nc.vector.tensor_scalar(FIRSTP[:, :], FIRST[:, :], PIOTA[:, 0:1], None, ALU.add))
            link(nc.vector.tensor_copy(FIRST_I[:, :], FIRST[0:1, :]))
            link(nc.vector.tensor_tensor(DREL[:, 0:SUPERS, :], DFv,
                                         FIRST[:, 0:SUPERS].unsqueeze(2).to_broadcast([P, SUPERS, GROUP]),
                                         ALU.subtract))
            link(nc.vector.tensor_copy(DREL[:, SUPERS, :], DREL[:, 0, :]))
            assert WIN == 3 * 32 and N // 32 < 512
            link(nc.vector.tensor_tensor(FA[:, 0, 0:SUPERS], MR[0:1, 0:SUPERS], FIRST[0:1, 0:SUPERS], ALU.subtract))
            wins = WINS_I[:, 0:SUPERS]
            link(nc.vector.tensor_copy(wins, FA[:, 0, 0:SUPERS]))
            link(nc.vector.tensor_single_scalar(wins, wins, 5, ALU.logical_shift_right))
            link(nc.vector.tensor_scalar(wins, wins, 171.0, None, ALU.mult))
            link(nc.vector.tensor_single_scalar(wins, wins, 9, ALU.logical_shift_right))
            link(nc.vector.tensor_scalar(wins, wins, 1.0, None, ALU.add))
            link(nc.vector.memset(FA[:, :, :], float(N)))
            link(nc.vector.tensor_reduce(FA[:, 0, 0:TURNS], FIRST[0:1, 0:SUPERS].rearrange("p (i h) -> p i h", h=SLOTS),
                                         AX.X, ALU.min))
            a = 0
            for k in (1, 2, 4, 8, 16, 32):
                link(nc.vector.tensor_tensor(FA[:, 1 - a, 0:TURNS], FA[:, a, 0:TURNS], FA[:, a, k:k + TURNS], ALU.min))
                a = 1 - a
            link(nc.vector.tensor_scalar(FA[:, 1 - a, 0:TURNS], FA[:, a, 0:TURNS], -(UNIT - 1) / 2, 1.0 / UNIT,
                                         ALU.add, ALU.mult))
            link(nc.vector.tensor_scalar_max(FA[:, a, 0:TURNS], FA[:, 1 - a, 0:TURNS], 0.0))
            link(nc.vector.tensor_copy(FRONT_I[:, 0:TURNS], FA[:, a, 0:TURNS]))
            link(nc.vector.memset(FRONT_I[:, 0:1], 0))
            turn_no = IOTA[0:1, 0:TURNS]
            room = 64
            here = slice(room, room + TURNS)
            link(nc.vector.memset(FA[:, :, :], float(N)))
            link(nc.vector.tensor_tensor(FA[:, 0, here], FRONT_I[:, :], turn_no, ALU.subtract))
            a = 0
            for k in (1, 2, 4, 8, 16, 32):
                link(nc.vector.tensor_tensor(FA[:, 1 - a, here], FA[:, a, here],
                                             FA[:, a, room - k:room - k + TURNS], ALU.min))
                a = 1 - a
            link(nc.vector.tensor_tensor(DONE_I[:, 1:], FA[:, a, here], turn_no, ALU.add))
            link(nc.vector.memset(DONE_I[:, 0:1], 0))
            dve.wait_ge(src_in, 16)
            dve.wait_ge(loaded, ALL_LOADED)
            link(nc.vector.tensor_scalar(DI, SRC[:, 0:CHUNKS], float(R), None, ALU.mult))
            link(nc.vector.tensor_tensor(IDX3[:, 0:CHUNKS], IDX3[:, 0:CHUNKS], DI, ALU.add))
            link(nc.vector.tensor_scalar(IDENT[:, :], IOTA[:, :], PIOTA[:, 0:1], None, ALU.is_equal))
            assert step[0] == TABLES_READY, step[0]
            dve.wait_ge(products, 1)
            link(nc.vector.tensor_copy(mu[:, :], NA[:, 0:H]))
            link(nc.vector.tensor_copy(u1[D:D + 1, :], NB[0:1, 0:H]))
            dve.sem_inc(mixed, 1)
            dve.sem_inc(added, 2)
            assert step[0] == PREP_READY, step[0]

            far = dve.alloc_register("dve_far")
            steps = dve.alloc_register("dve_steps")
            more = dve.alloc_register("dve_more")
            for reg in (far, steps, more):
                dve.reg_mov(reg, 0)

            def far_link(ins):
                ins.then_inc(far_step, 1)
                dve.reg_add(steps, steps, 1)
                dve.wait_ge(far_step, dve.snap(steps))
                dve.sem_inc(dve_go, 1)

            def one_hot(b, d):
                return nc.vector.tensor_tensor(OH[:, b, :, :], IOTA[:, 0:WIN].unsqueeze(1).to_broadcast([P, GROUP, WIN]),
                                               d.unsqueeze(2).to_broadcast([P, GROUP, WIN]), ALU.is_equal)

            def targets(s):
                return DREL[:, bass.ds(s, 1), :].rearrange("p a j -> p (a j)")

            def add_window(b, m, at):
                dst = AGG[0:m, bass.ds(at, WIN)]
                return nc.vector.tensor_tensor(dst, dst, PAG[b][0:m, 0:WIN], ALU.add)

            def add_super(p, s, h, m):
                b = h % 2
                w0 = dve.value_load(FIRST_I[0:1, bass.ds(s, 1)], min_val=0, max_val=N)
                n = dve.value_load(WINS_I[0:1, bass.ds(s, 1)], min_val=1, max_val=P + 4)
                dve.wait_ge(summed, s + (SUPERS * p + 1))
                dve.wait_ge(added, s + (SUPERS * p + 2))
                add_window(b, m, w0).then_inc(added, 1)
                with dve.If(n > 1):
                    dve.wait_ge(added, s + (SUPERS * p + 3))
                    far_link(nc.vector.tensor_scalar(DCUR[:, :], targets(s), 0.0, None, ALU.add))
                    with dve.Fori(1, n) as it:
                        far_link(nc.vector.tensor_scalar(DCUR[:, :], DCUR[:, :], -float(WIN), None, ALU.add))
                        one_hot(b, DCUR[:, :]).then_inc(far_hot, 1)
                        dve.reg_add(far, far, 1)
                        dve.wait_ge(far_summed, dve.snap(far))
                        far_link(add_window(b, m, within(w0 + it * WIN)))
                if p != 1:
                    release(h)

            def release(h):
                nc.vector.memset(TICK[:, h:h + 1], 0.0).then_inc(released, 1)

            def hot_T(t, b, uses, first=False):
                dve.wait_ge(ef_in[b], uses * 48)
                if not first:
                    dve.wait_ge(pre_done, t)
                dve.sem_inc(dve_go, 1)
                nc.vector.tensor_scalar(MIXT[0:WIN, b, :], DROW[:, b, :], FIRSTP[0:WIN, bass.ds(t, 1)], None,
                                        ALU.is_equal).then_inc(hotT_ready, 1)

            def more_hot_T(t, b):
                n = dve.value_load(WINS_I[0:1, bass.ds(t, 1)], min_val=1, max_val=P + 4)
                with dve.If(n > 1):
                    dve.wait_ge(pre_done, t + 2)
                    far_link(nc.vector.tensor_scalar(FCUR[:, :], FIRSTP[:, bass.ds(t, 1)], 0.0, None, ALU.add))
                    with dve.Fori(1, n) as it:
                        far_link(nc.vector.tensor_scalar(FCUR[:, :], FCUR[:, :], float(WIN), None, ALU.add))
                        dve.reg_add(more, more, 1)
                        dve.wait_ge(more_done, dve.snap(more))
                        nc.vector.tensor_scalar(MIXT[0:WIN, b, :], DROW[:, b, :], FCUR[0:WIN, 0:1], None,
                                                ALU.is_equal).then_inc(more_hot, 1)
                    dve.wait_ge(more_done, dve.snap(dve.snap(more) + 1))
                    dve.sem_inc(dve_go, 1)

            def move(dst, src_):
                return nc.vector.tensor_scalar(dst, src_, 1.0, None, ALU.mult)

            def steps_of(p, u, before=0):
                count = [before]

                def run(*instructions):
                    count[0] += 1
                    instructions[-1].then_inc(chain[p], 1)
                    dve.wait_ge(chain[p], u * CHAIN[p] + count[0])

                def done():
                    assert count[0] == CHAIN[p], (p, count[0])
                return run, done

            def fetch(p, u, m):
                move(Z[0:m, :], AGG[0:m, bass.ds(u * UNIT, UNIT)])
                if p in (2, 3):
                    move(IU[0:HALF, :], INV[0:HALF, bass.ds(u * 2, 2)])
                last = move(XU[0:HALF, :, :] if p else XU[0:HALF, :, 0:D],
                            X[0:HALF, bass.ds(u * 2, 2), :] if p else X[0:HALF, bass.ds(u * 2, 2), 0:D])
                last.then_inc(staged[p], 1)
                dve.wait_ge(staged[p], u + 1)
                nc.vector.tensor_scalar(AGG[:, bass.ds(u * UNIT, UNIT)], ZERO[:, :], 0.0, None, ALU.add)\
                  .then_inc(cleared[p], 1)

            def layer_norm(p, u, run, n=1, k=0):
                run(nc.vector.bn_stats(ST6[0:HALF, 0, :], Y[0:HALF, 0, 0:D]),
                    nc.vector.bn_stats(ST6[0:HALF, 1, :], Y[0:HALF, 1, 0:D]))
                dve.sem_inc(dve_go, 1)
                run(nc.vector.bn_aggr(MV[0:HALF, 0, :], ST6[0:HALF, 0, :]),
                    nc.vector.bn_aggr(MV[0:HALF, 1, :], ST6[0:HALF, 1, :]))
                nc.vector.tensor_scalar(VE[0:HALF, :], MV[0:HALF, :, 1], LN_EPS, None, ALU.add).then_inc(var_ready[p], 1)
                dve.wait_ge(root_ready[p], u * n + (k + 1))
                run(nc.vector.reciprocal(RS[0:HALF, :], SQ[0:HALF, :]))
                if p in (1, 4):
                    dve.wait_ge(stored[p], u * STORE[p] + STORE[p])
                for a_ in range(2):
                    last = nc.vector.tensor_scalar(XS[0:HALF, a_, :], Y[0:HALF, a_, 0:D], MV[0:HALF, a_, 0:1],
                                                   RS[0:HALF, a_:a_ + 1], ALU.subtract, ALU.mult)
                last.then_inc(x_new[p], 1)
                if p < 4:
                    dve.wait_ge(x_new[p], u + 1)
                    move(X[0:HALF, bass.ds(u * 2, 2), 0:D], XS[0:HALF, :, :]).then_inc(x_kept[p], 1)

            def inverse_norm(p, u, run, w, n, k):
                y = Y[0:HALF, :, 0:w]
                run(nc.vector.tensor_tensor(Y2[0:HALF, :, 0:w], y, y, ALU.mult))
                run(nc.vector.tensor_reduce(SS[0:HALF, :], Y2[0:HALF, :, 0:w], AX.X, ALU.add))
                nc.vector.tensor_scalar(VE[0:HALF, :], SS[0:HALF, :], NORM_FLOOR_SQ, None, ALU.max)\
                  .then_inc(var_ready[p], 1)
                dve.wait_ge(root_ready[p], u * n + (k + 1))
                run(nc.vector.reciprocal(RS[0:HALF, :], SQ[0:HALF, :]))

            def halves(t, w=D):
                return t.rearrange("p (a c) -> p a c", c=w)

            def node0(u, stage):
                if stage == 0:
                    fetch(0, u, D + 1)
                if stage == 1:
                    run, done = steps_of(0, u)
                    dve.wait_ge(l0_hidden, u + 1)
                    for a_ in range(2):
                        last = nc.vector.tensor_scalar(NEG[:, a_ * UNIT:(a_ + 1) * UNIT],
                                                       NA[:, a_ * UNIT:(a_ + 1) * UNIT],
                                                       b1c[:, a_:a_ + 1], 0.0, ALU.add, ALU.min)
                    last.then_inc(l0_neg, 1)
                    degree = NB[0:HALF, 508:510]
                    move(X[0:HALF, bass.ds(u * 2, 2), D], degree)
                    run(nc.vector.tensor_scalar(IU[0:HALF, :], degree, 1.0, None, ALU.max))
                    run(nc.vector.reciprocal(SS[0:HALF, :], IU[0:HALF, :]))
                    move(INV[0:HALF, bass.ds(u * 2, 2)], SS[0:HALF, :])
                    dve.wait_ge(l0_pos, u + 1)
                    dve.wait_ge(l0_exp, u + 1)
                    nc.vector.scalar_tensor_tensor(NEG[:, :], NEG[:, :], -1.0, POS[:, :], ALU.add, ALU.add)\
                      .then_inc(l0_elu, 1)
                if stage == 2:
                    run, done = steps_of(0, u, 2)
                    dve.wait_ge(y_ready[0], u + 1)
                    run(nc.vector.tensor_tensor(Y[0:HALF, :, 0:D], halves(NB[0:HALF, 0:2 * D]), XU[0:HALF, :, 0:D],
                                                ALU.add))
                    layer_norm(0, u, run)
                    done()

            def node1(u, stage):
                if stage == 0:
                    fetch(1, u, H)
                if stage == 3:
                    run, done = steps_of(1, u)
                    dve.wait_ge(y_ready[1], u + 1)
                    run(nc.vector.tensor_tensor(Y[0:HALF, :, 0:D], halves(NB[0:HALF, 0:2 * D]), XU[0:HALF, :, 0:D],
                                                ALU.add))
                    layer_norm(1, u, run)
                    done()

            def node2(u, stage):
                if stage == 0:
                    fetch(2, u, D)
                if stage == 2:
                    run, done = steps_of(2, u)
                    dve.wait_ge(l2_scaled, u + 1)
                    run(nc.vector.tensor_tensor(Y[0:HALF, :, :], halves(NB[0:HALF, 0:2 * H], H), Y2[0:HALF, :, :],
                                                ALU.add))
                    inverse_norm(2, u, run, H, 1, 0)
                    for a_ in range(2):
                        last = nc.vector.tensor_scalar(Y2[0:HALF, a_, :], Y[0:HALF, a_, :], RS[0:HALF, a_:a_ + 1],
                                                       None, ALU.mult)
                    last.then_inc(l2_normed, 1)
                    done()
                if stage == 3:
                    dve.wait_ge(l2_kept, u + 1)
                    dve.sem_inc(dve_go, 1)
                    nc.vector.bn_stats(BST[:, bass.ds(u, 1), :].rearrange("p a c -> p (a c)"), NA[:, 0:UNIT])\
                      .then_inc(l2_stats, 1)

            def batch_norm_table():
                dve.wait_ge(l2_stats, UNITS)
                nc.vector.bn_aggr(BMV[:, :], BST[:, :, :].rearrange("p u c -> p (u c)")).then_inc(bn_step, 1)
                dve.wait_ge(bn_step, 1)
                nc.vector.tensor_scalar(BT[:, 0:1], BMV[:, 1:2], BN_EPS, None, ALU.add).then_inc(bn_var, 1)
                dve.wait_ge(bn_root, 1)
                nc.vector.reciprocal(BT[:, 2:3], BT[:, 1:2]).then_inc(bn_step, 1)
                dve.wait_ge(bn_step, 2)
                nc.vector.tensor_tensor(BSC[:, :], BT[:, 2:3], gam[:, :], ALU.mult).then_inc(bn_step, 1)
                dve.wait_ge(bn_step, 3)
                nc.vector.tensor_tensor(BT[:, 3:4], BMV[:, 0:1], BSC[:, :], ALU.mult).then_inc(bn_step, 1)
                dve.wait_ge(bn_step, 4)
                nc.vector.tensor_tensor(BSH[:, :], bet[:, :], BT[:, 3:4], ALU.subtract).then_inc(bn_ready, 1)

                def rows_out_of_psum(u, b, first):
                    dve.wait_ge(bn_map, u + 3)
                    if not first:
                        dve.wait_ge(bn_stored[b], (u - b) * 8)
                    move(STG[0:HALF, b, 0:2 * D], (NA, NB)[b][0:HALF, 0:2 * D]).then_inc(bn_out, 1)

                for b in range(2):
                    rows_out_of_psum(b, b, True)
                with dve.Fori(1, UNITS // 2) as i:
                    for b in range(2):
                        rows_out_of_psum(i * 2 + b, b, False)

            def node3(u, stage):
                if stage == 0:
                    fetch(3, u, D)
                if stage == 1:
                    run, done = steps_of(3, u)
                    dve.wait_ge(l3_scaled, u + 1)
                    run(nc.vector.tensor_tensor(Y[0:HALF, :, 0:D], halves(NA[0:HALF, 0:2 * D]), Y2[0:HALF, :, 0:D],
                                                ALU.add))
                    dve.sem_inc(dve_go, 1)
                if stage == 2:
                    run, done = steps_of(3, u, 1)
                    for k in range(2):
                        inverse_norm(3, u, run, D, 3, k)
                        run(*[nc.vector.scalar_tensor_tensor(Y[0:HALF, a_, 0:D], Y[0:HALF, a_, 0:D],
                                                             RS[0:HALF, a_:a_ + 1], XU[0:HALF, a_, 0:D],
                                                             ALU.mult, ALU.add) for a_ in range(2)])
                    layer_norm(3, u, run, 3, 2)
                    done()

            def node4(u, stage):
                if stage == 0:
                    fetch(4, u, D)
                if stage == 2:
                    run, done = steps_of(4, u)
                    dve.wait_ge(y_ready[4], u + 1)
                    run(nc.vector.tensor_tensor(Y[0:HALF, :, 0:D], halves(NB[0:HALF, 0:2 * D]), XU[0:HALF, :, 0:D],
                                                ALU.add))
                    layer_norm(4, u, run)
                    done()

            node = [node0, node1, node2, node3, node4]
            one_hot(0, targets(0)).then_inc(onehot_ready, 1)
            for p in range(LAYERS):
                m = (D + 1, H, D, D, D)[p]
                if p:
                    dve.wait_ge(cleared[p - 1], UNITS)
                    if p != 3:
                        dve.wait_ge(x_kept[p - 1], UNITS)
                    dve.sem_inc(dve_go, 1)
                if p == 1:
                    hot_T(0, 0, 1, first=True)
                    more_hot_T(0, 0)
                with dve.Fori(0, TURNS) as i:
                    turn_units = unit_of_turn(dve, i)
                    for h in range(SLOTS):
                        if p == 1:
                            hot_T(i * SLOTS + (h + 1), (h + 1) % 2, i * (SLOTS // 2) + ((h + 1) // 2 + 1))
                            dve.wait_ge(pre_done, i * SLOTS + (h + 2))
                            dve.wait_ge(gathered[h], slot_gathered(p, i))
                            nc.vector.tensor_tensor(HID[:, h % 2, :], PH[h % 2][:, :],
                                                    G[:, h, :, :].rearrange("p j c -> p (j c)"), ALU.add)\
                              .then_inc(mixed, 1)
                            release(h)
                        if h:
                            add_super(p, i * SLOTS + (h - 1), h - 1, m)
                        else:
                            with dve.If(i > 0):
                                add_super(p, nc.s_assert_within(i * SLOTS - 1, 0, SUPERS - 1), SLOTS - 1, m)
                        one_hot((h + 1) % 2, targets(i * SLOTS + (h + 1))).then_inc(onehot_ready, 1)
                        if p == 1:
                            more_hot_T(i * SLOTS + (h + 1), (h + 1) % 2)
                        if h == 0:
                            dve.wait_ge(added, i * SLOTS + (SUPERS * p + 2))
                            dve.sem_inc(dve_go, 1)
                        stage_of_turn(dve, turn_units, node[p], h)
                add_super(p, SUPERS - 1, SLOTS - 1, m)
                dve.wait_ge(added, SUPERS * (p + 1) + 2)
                last_units(dve, node[p])
                if p == 2:
                    batch_norm_table()

        @block.tensor
        def _(pe):
            def mm(dst, lhsT, rhs, start=True, stop=True):
                return nc.tensor.matmul(dst, lhsT, rhs, start=start, stop=stop, skip_group_check=True)

            def with_bias(dst, lhsT, rhs, bias):
                mm(dst, lhsT, rhs, stop=False)
                return mm(dst, ONES[0:1, 0:HALF], bias, start=False)

            def half(a):
                return slice(a * HALF, (a + 1) * HALF)

            pe.sem_inc(more_done, 1)
            pe.sem_inc(pre_done, 1)
            pe.sem_inc(bn_map, 2)
            pe.sem_inc(bn_out, 2)
            pe.wait_ge(loaded, ALL_LOADED)
            mm(NA[:, 0:H], mw2T[:, :], uw1b[:, :])
            mm(NB[0:1, 0:H], mb2c[:, :], uw1b[:, :]).then_inc(products, 1)
            pe.wait_ge(prep, PREP_READY)
            pe.sem_inc(pe_go, 1)
            far = pe.alloc_register("pe_far")
            more = pe.alloc_register("pe_more")
            for reg in (far, more):
                pe.reg_mov(reg, 0)

            def sum_window(p, h, m):
                msg = HID[:, h % 2, :].rearrange("p (j c) -> p j c", j=GROUP) if p == 1 else G[:, h, :, :]
                for j in range(GROUP):
                    last = mm(PAG[h % 2][0:m, 0:WIN], msg[:, j, 0:m], OH[:, h % 2, j, :], j == 0, j == GROUP - 1)
                return last

            def sum_super(p, i, h, n, m):
                pe.wait_ge(onehot_ready, i * SLOTS + (SUPERS * p + h + 1))
                pe.wait_ge(added, i * SLOTS + (SUPERS * p + h + 1))
                if p == 1:
                    pe.wait_ge(relu_done, i * SLOTS + (h + 1))
                else:
                    pe.wait_ge(gathered[h], i * (16 * GROUP) + 16 * GROUP * (TURNS * p + 1))
                sum_window(p, h, m).then_inc(summed, 1)
                with pe.If(n > 1):
                    with pe.Fori(1, n) as it:
                        pe.reg_add(far, far, 1)
                        pe.wait_ge(far_hot, pe.snap(far))
                        sum_window(p, h, m).then_inc(far_summed, 1)

            def pre(t, b, uses, first=False):
                n = pe.value_load(WINS_I[0:1, bass.ds(t, 1)], min_val=1, max_val=P + 4)
                pe.wait_ge(ef_in[b], uses * 48)
                pe.wait_ge(hotT_ready, t + 1)
                if not first:
                    pe.wait_ge(mixed, t)
                pe.sem_inc(pe_go, 1)
                for j in range(GROUP):
                    c = slice(j * P, (j + 1) * P)
                    last = mm(PH[b][:, c], MIXT[:, b, c], MIXW[:, b, :], j % 4 == 0, j % 4 == 3)
                last.then_inc(pre_done, 1)
                with pe.If(n > 1):
                    with pe.Fori(1, n) as it:
                        pe.reg_add(more, more, 1)
                        window = pe.snap(more)
                        landed = pe.snap(window * 16)
                        pe.wait_ge(more_in, landed)
                        pe.wait_ge(more_hot, window)
                        for j in range(GROUP):
                            c = slice(j * P, (j + 1) * P)
                            last = mm(PH[b][:, c], MIXT[0:WIN, b, c], MOREW, False, j % 4 == 3)
                        last.then_inc(more_done, 1)

            def flip(p, tile, m):
                for a in range(2):
                    last = mm(PT[0:m, half(a)], tile[0:HALF, a, 0:m], IDENT[0:HALF, 0:HALF])
                last.then_inc(flipped[p], 1)

            def node0(u, stage):
                if stage == 1:
                    pe.wait_ge(staged[0], u + 1)
                    for a in range(2):
                        mm(NA[:, a * UNIT:(a + 1) * UNIT], w1[:, a * H:(a + 1) * H], Z[0:D, :])
                        last = mm(NB[0:HALF, 508 + a:509 + a], Z[D:D + 1, half(a)], ONES[D:D + 1, 0:1])
                    last.then_inc(l0_hidden, 1)
                if stage == 2:
                    pe.wait_ge(l0_elu, u + 1)
                    for a in range(2):
                        dst = NB[0:HALF, a * D:(a + 1) * D]
                        mm(dst, NEG[:, half(a)], w2[:, 0, :], stop=False)
                        mm(dst, NEG[:, UNIT + a * HALF:UNIT + (a + 1) * HALF], w2[:, 1, :], False, False)
                        last = mm(dst, ONES[0:1, 0:HALF], b2r, False)
                    last.then_inc(y_ready[0], 1)
                if stage == 3:
                    pe.wait_ge(x_new[0], u + 1)
                    flip(0, XS, D)
                    pe.wait_ge(flip_copied[0], u + 1)
                    for a in range(2):
                        last = with_bias(NA[0:HALF, a * 2 * H:(a + 1) * 2 * H], XT[0:D, half(a)], wfn[:, :], mb1r)
                    last.then_inc(l0_maps, 1)
                    pe.wait_ge(l0_maps_copied, u + 1)
                    pe.sem_inc(pe_go, 1)

            def node1(u, stage):
                if stage == 1:
                    pe.wait_ge(staged[1], u + 1)
                    flip(1, XU, D + 1)
                if stage == 2:
                    pe.wait_ge(flip_copied[1], u + 1)
                    mm(NA[:, 0:UNIT], u1[:, :], XT[:, :], stop=False)
                    mm(NA[:, 0:UNIT], mu[:, :], Z[:, :], False).then_inc(l1_hidden, 1)
                if stage == 3:
                    pe.wait_ge(l1_relu, u + 1)
                    for a in range(2):
                        last = with_bias(NB[0:HALF, a * D:(a + 1) * D], POS[:, half(a)], uw2[:, :], ub2r)
                    last.then_inc(y_ready[1], 1)

            def node2(u, stage):
                if stage == 1:
                    pe.wait_ge(staged[2], u + 1)
                    flip(2, XU, D)
                if stage == 2:
                    pe.wait_ge(flip_copied[2], u + 1)
                    for a in range(2):
                        mm(NA[0:HALF, a * H:(a + 1) * H], Z[0:D, half(a)], wl1[:, :])
                        last = with_bias(NB[0:HALF, a * H:(a + 1) * H], XT[0:D, half(a)], wr1[:, :], sb1r)
                    last.then_inc(l2_products, 1)
                if stage == 3:
                    pe.wait_ge(l2_normed, u + 1)
                    for a in range(2):
                        last = mm(NA[:, half(a)], Y2[0:HALF, a, :], IDENT[0:HALF, 0:HALF])
                    last.then_inc(l2_flipped, 1)

            def batch_norm_table():
                with pe.Fori(0, UNITS // 2) as i:
                    for b in range(2):
                        pe.wait_ge(bn_hot, i * 2 + (b + 1))
                        pe.wait_ge(bn_out, i * 2 + (b + 1))
                        for a in range(2):
                            last = mm((NA, NB)[b][0:HALF, a * D:(a + 1) * D], HB[:, b, half(a)], wl2[:, :])
                        last.then_inc(bn_map, 1)

            def node3(u, stage):
                if stage == 1:
                    pe.wait_ge(staged[3], u + 1)
                    pe.wait_ge(l3_hot, u + 1)
                    for a in range(2):
                        mm(NB[0:HALF, a * D:(a + 1) * D], Z[0:D, half(a)], IDENT[0:D, 0:D])
                        last = with_bias(NA[0:HALF, a * D:(a + 1) * D], HB[:, 0, half(a)], wr2[:, :], sb2r)
                    last.then_inc(l3_products, 1)
                if stage == 3:
                    pe.wait_ge(x_new[3], u + 1)
                    flip(3, XS, D)
                    pe.wait_ge(flip_copied[3], u + 1)
                    for k in range(4):
                        if k >= 2:
                            pe.wait_ge(l3_map_copied, u * 4 + (k - 1))
                        mm((NA, NB)[k % 2][0:HALF, :], XT[0:D, half(k // 2)],
                           wrel[:, (k % 2) * 512:(k % 2) * 512 + 512]).then_inc(l3_map, 1)

            def node4(u, stage):
                if stage == 1:
                    pe.wait_ge(staged[4], u + 1)
                    for a in range(2):
                        last = mm(NB[0:HALF, a * D:(a + 1) * D], Z[0:D, half(a)], IDENT[0:D, 0:D])
                    last.then_inc(y_ready[4], 1)

            node = [node0, node1, node2, node3, node4]
            for p in range(LAYERS):
                m = (D + 1, H, D, D, D)[p]
                if p == 1:
                    pre(0, 0, 1, first=True)
                with pe.Fori(0, TURNS) as i:
                    turn_units = unit_of_turn(pe, i)
                    for h in range(SLOTS):
                        n = pe.value_load(WINS_I[0:1, bass.ds(i * SLOTS + h, 1)], min_val=1, max_val=P + 4)
                        if p == 1:
                            pre(i * SLOTS + (h + 1), (h + 1) % 2, i * (SLOTS // 2) + ((h + 1) // 2 + 1))
                        sum_super(p, i, h, n, m)
                        stage_of_turn(pe, turn_units, node[p], h)
                last_units(pe, node[p])
                if p == 2:
                    batch_norm_table()


def kernel(x, src, dst, edge_attr_32, edge_type_16, L0_gnn_W1, L0_gnn_b1, L0_gnn_W2, L0_gnn_b2,
           L1_gnn_mW1, L1_gnn_mb1, L1_gnn_mW2, L1_gnn_mb2, L1_gnn_uW1, L1_gnn_ub1, L1_gnn_uW2, L1_gnn_ub2,
           L2_gnn_Wl1, L2_gnn_Wr1, L2_gnn_b1, L2_gnn_gamma1, L2_gnn_beta1, L2_gnn_Wl2, L2_gnn_Wr2, L2_gnn_b2,
           L3_gnn_weight):
    import numpy as np
    import concourse.bacc as bacc
    from concourse.bass_utils import run_bass_kernel_spmd

    def padded(a, last, fill):
        a = np.asarray(a)
        out = np.full(a.shape[:-1] + (last,), fill, a.dtype)
        out[..., :a.shape[-1]] = a
        return out

    def by_chunk(a, fill):
        return padded(a, CHUNKS * P, fill).reshape(CHUNKS, P).T

    def column(a):
        return np.asarray(a).reshape(-1, 1)

    def row(a):
        return np.asarray(a).reshape(1, -1)

    arrays = {
        "x": x, "xT": np.asarray(x).T,
        "src_c": by_chunk(src, 0), "dst_c": by_chunk(dst, N), "dst_r": padded(dst, CHUNKS * P, N).reshape(P, CHUNKS),
        "type_c": by_chunk(edge_type_16, 0), "efT": padded(np.asarray(edge_attr_32).T, (SUPERS + 2) * SUPER, 0),
        "W1": L0_gnn_W1, "b1": np.asarray(L0_gnn_b1).reshape(2, P).T, "W2": L0_gnn_W2, "b2": row(L0_gnn_b2),
        "mW1": L1_gnn_mW1, "mb1": row(L1_gnn_mb1), "mW2T": np.asarray(L1_gnn_mW2).T, "mb2": column(L1_gnn_mb2),
        "uW1": L1_gnn_uW1, "ub1": column(L1_gnn_ub1), "uW2": L1_gnn_uW2, "ub2": row(L1_gnn_ub2),
        "Wl1": L2_gnn_Wl1, "Wr1": L2_gnn_Wr1, "sb1": row(L2_gnn_b1), "gamma": column(L2_gnn_gamma1),
        "beta": column(L2_gnn_beta1), "Wl2": L2_gnn_Wl2, "Wr2": L2_gnn_Wr2, "sb2": row(L2_gnn_b2),
        "Wrel": np.asarray(L3_gnn_weight).transpose(1, 0, 2).reshape(D, R * D),
    }
    arrays = {name: np.ascontiguousarray(a) for name, a in arrays.items()}
    nc = bacc.Bacc("TRN2", target_bir_lowering=False, num_devices=1)
    args = [nc.dram_tensor(f"in_{name}", a.shape, mybir.dt.from_np(a.dtype), kind="ExternalInput").ap()
            for name, a in arrays.items()]
    out = nc.dram_tensor("out", (N, D), F32, kind="ExternalOutput").ap()
    gnn_kernel(nc, *args, out)
    r = run_bass_kernel_spmd(nc, [{f"in_{name}": a for name, a in arrays.items()}], core_ids=[0])
    return r.results[0]["out"]
```

```python
from contextlib import ExitStack

import concourse.bass as bass
from concourse import mybir
from concourse.alu_op_type import AluOpType as ALU

F32 = mybir.dt.float32
I32 = mybir.dt.int32
I16 = mybir.dt.int16
ACT = mybir.ActivationFunctionType
AX = mybir.AxisListType

N = 12500
E = 200000
D = 64
H = 128
DE = 32
R = 16
P = 128
GROUP = 8
SUPER = GROUP * P
SLOTS = 4
SUPERS = -(-E // (SUPER * SLOTS)) * SLOTS
TURNS = SUPERS // SLOTS
CHUNKS = SUPERS * GROUP
UNIT = 250
HALF = UNIT // 2
UNITS = N // UNIT
WIN = P - DE
NPAD = N + P + 44
LAYERS = 5
LN_EPS = 1e-5
BN_EPS = 1e-5
NORM_FLOOR_SQ = 1e-24
RMAX = bass.bass_isa.ReduceOp.max
SPANS_READY, ROWS_READY, PREP_READY, TABLES_READY = 5, 31, 33, 35
ROWS_OUT = 4 * 16
CHAIN = [6, 4, 4, 12, 4]


def gnn_kernel(nc, x, xT, src_c, dst_c, dst_r, type_c, efT, W1, b1, W2, b2, mW1, mb1, mW2T, mb2,
               uW1, ub1, uW2, ub2, Wl1, Wr1, sb1, gamma, beta, Wl2, Wr2, sb2, Wrel, out):
    ctx = ExitStack()
    with ctx:
        def sb(name, shape, dt=F32):
            return ctx.enter_context(nc.sbuf_tensor(name, shape, dt))

        def sem(name):
            return ctx.enter_context(nc.semaphore(name))

        def dram(name, shape, dt=F32):
            return nc.dram_tensor(name, shape, dt, kind="Internal").ap()

        near_tab = dram("near_tab", [NPAD, H])
        far_tab = dram("far_tab", [N, H])
        x2_tab = dram("x2_tab", [N, D])
        h_tab = dram("h_tab", [N, H])
        rel_tab = dram("rel_tab", [N * R, D])
        dst_rows = dram("dst_rows", [1, (SUPERS + 2) * SUPER], I16)

        X = sb("X", [P, 2 * UNITS, D + 1])
        AGG = sb("AGG", [P, NPAD])
        HT = sb("HT", [P, N])
        INV = sb("INV", [P, 2 * UNITS])
        SRC = sb("SRC", [P, CHUNKS + SLOTS * GROUP], I32)
        IDX3 = sb("IDX3", [P, CHUNKS + SLOTS * GROUP], I32)
        DREL = sb("DREL", [P, SUPERS + 1, GROUP])
        FIRST = sb("FIRST", [P, SUPERS + 2])
        FIRSTP = sb("FIRSTP", [P, SUPERS + 2])
        FIRST_I = sb("FIRST_I", [1, SUPERS + 2], I32)
        WINS_I = sb("WINS_I", [1, SUPERS + 2], I32)
        DONE_I = sb("DONE_I", [1, TURNS + 1], I32)
        IDXB = sb("IDXB", [P, SLOTS, GROUP], I32)
        G = sb("G", [P, SLOTS, GROUP, P])
        OH = sb("OH", [P, 2, GROUP, WIN])
        DCUR = sb("DCUR", [P, GROUP])
        FCUR = sb("FCUR", [P, 1])
        TICK = sb("TICK", [1, SLOTS])
        MIXT = HT[:, 0:2 * SUPER].rearrange("p (b e) -> p b e", b=2)
        o = 2 * SUPER
        MIXW = HT[:, o:o + 2 * H].rearrange("p (b n) -> p b n", b=2)
        o += 2 * H
        MOREW = HT[0:WIN, o:o + H]
        o += H
        HID = HT[:, o:o + 2 * SUPER].rearrange("p (b e) -> p b e", b=2)
        o += 2 * SUPER
        DROW = HT[0:WIN, o:o + SUPER].bitcast(I16).rearrange("p (b e) -> p b e", b=2)
        o += SUPER
        DI = HT[:, o:o + CHUNKS].bitcast(I32)
        o += CHUNKS
        DF = HT[:, o:o + CHUNKS]
        o += CHUNKS
        T1 = HT[:, o:o + CHUNKS].bitcast(I32)
        o += CHUNKS
        DST16 = HT[:, o:o + CHUNKS // 2].bitcast(I16)
        FA = sb("FA", [1, 2, SUPERS])
        IOTA = sb("IOTA", [P, P])
        PIOTA = sb("PIOTA", [P, 1])
        IDENT = sb("IDENT", [P, P])
        ONES = sb("ONES", [P, HALF])
        ZERO = sb("ZERO", [P, UNIT])
        w1 = sb("w1", [D, 2 * H])
        b1c = sb("b1c", [P, 2])
        w2 = sb("w2", [P, 2, D])
        rows = sb("rows", [1, 3 * D + 3 * H])
        b2r, ub2r, sb2r = rows[:, 0:D], rows[:, D:2 * D], rows[:, 2 * D:3 * D]
        mb1r = rows[:, 3 * D:3 * D + 2 * H]
        sb1r = rows[:, 3 * D + 2 * H:3 * D + 3 * H]
        wfn = sb("wfn", [D, 2 * H])
        mw2T = sb("mw2T", [D, H])
        mb2c = sb("mb2c", [D, 1])
        uw1b = sb("uw1b", [D, H])
        u1 = sb("u1", [D + 1, H])
        mu = sb("mu", [H, H])
        ub1c = sb("ub1c", [P, 1])
        uw2 = sb("uw2", [P, D])
        wl1 = sb("wl1", [D, H])
        wr1 = sb("wr1", [D, H])
        gam = sb("gam", [P, 1])
        bet = sb("bet", [P, 1])
        wl2 = sb("wl2", [P, D])
        wr2 = sb("wr2", [P, D])
        wrel = sb("wrel", [D, R * D])
        Z = sb("Z", [P, UNIT])
        XU = sb("XU", [P, 2, D + 1])
        IU = sb("IU", [P, 2])
        XT = sb("XT", [D + 1, UNIT])
        POS = sb("POS", [P, 2 * UNIT])
        NEG = sb("NEG", [P, 2 * UNIT])
        HB = POS[:, 0:UNIT]
        Y = sb("Y", [P, 2, H])
        Y2 = sb("Y2", [P, 2, H])
        XS = sb("XS", [P, 2, D])
        ST6 = sb("ST6", [P, 2, 6])
        MV = sb("MV", [P, 2, 2])
        SS = sb("SS", [P, 2])
        VE = sb("VE", [P, 2])
        SQ = sb("SQ", [P, 2])
        RS = sb("RS", [P, 2])
        STG = sb("STG", [P, 2, R * D])
        GH = STG[:, 0, 0:2 * H].rearrange("p (a c) -> p a c", a=2)
        MM = STG[:, 0, 0:2 * SUPERS]
        MR = STG[:, 1, 0:2 * SUPERS]
        BST = sb("BST", [P, UNITS, 6])
        BMV = sb("BMV", [P, 2])
        BT = sb("BT", [P, 4])
        BSC = sb("BSC", [P, 1])
        BSH = sb("BSH", [P, 1])
        BC = sb("BC", [P, 3])
        CROW = sb("CROW", [P, H])
        GROW = sb("GROW", [P, H])

        def pb(name, shape):
            return ctx.enter_context(nc.psum_tensor(name, shape, F32))

        PH = [pb("PH0", [P, SUPER]), pb("PH1", [P, SUPER])]
        PAG = [pb("PAG0", [P, 512]), pb("PAG1", [P, 512])]
        NA = pb("NA", [P, 512])
        NB = pb("NB", [P, 512])
        PT = NB[:, 256:256 + UNIT]

        x_in = sem("x_in")
        src_in = sem("src_in")
        rows_in = sem("rows_in")
        x_loaded = sem("x_loaded")
        loaded = sem("loaded")
        agg_zero = sem("agg_zero")
        zero_ready = sem("zero_ready")
        const_pool = sem("const_pool")
        prep = sem("prep")
        spans_out = sem("spans_out")
        rows_out = sem("rows_out")
        products = sem("products")
        idx_staged = [sem(f"idx_staged{h}") for h in range(SLOTS)]
        gathered = [sem(f"gathered{h}") for h in range(SLOTS)]
        released = sem("released")
        onehot_ready = sem("onehot_ready")
        summed = sem("summed")
        added = sem("added")
        pool_go, act_go, dve_go = sem("pool_go"), sem("act_go"), sem("dve_go")
        pe_go, sp_go = sem("pe_go"), sem("sp_go")
        far_hot = sem("far_hot")
        far_summed = sem("far_summed")
        far_step = sem("far_step")
        ef_in = [sem("ef_in0"), sem("ef_in1")]
        hotT_ready = sem("hotT_ready")
        pre_done = sem("pre_done")
        mixed = sem("mixed")
        relu_done = sem("relu_done")
        more_in = sem("more_in")
        more_hot = sem("more_hot")
        more_done = sem("more_done")
        staged = [sem(f"staged{p}") for p in range(LAYERS)]
        cleared = [sem(f"cleared{p}") for p in range(LAYERS)]
        chain = [sem(f"chain{p}") for p in range(LAYERS)]
        y_ready = [sem(f"y_ready{p}") for p in range(LAYERS)]
        var_ready = [sem(f"var_ready{p}") for p in range(LAYERS)]
        root_ready = [sem(f"root_ready{p}") for p in range(LAYERS)]
        x_new = [sem(f"x_new{p}") for p in range(LAYERS)]
        x_kept = [sem(f"x_kept{p}") for p in range(LAYERS)]
        flipped = [sem(f"flipped{p}") for p in range(LAYERS)]
        flip_copied = [sem(f"flip_copied{p}") for p in range(LAYERS)]
        stored = [sem(f"stored{p}") for p in range(LAYERS)]
        l0_hidden, l0_pos, l0_neg = sem("l0_hidden"), sem("l0_pos"), sem("l0_neg")
        l0_exp, l0_elu = sem("l0_exp"), sem("l0_elu")
        l0_maps, l0_maps_copied = sem("l0_maps"), sem("l0_maps_copied")
        l1_hidden, l1_relu = sem("l1_hidden"), sem("l1_relu")
        l2_products, l2_scaled, l2_normed = sem("l2_products"), sem("l2_scaled"), sem("l2_normed")
        h_ready = sem("h_ready")
        l2_flipped, l2_kept, l2_stats = sem("l2_flipped"), sem("l2_kept"), sem("l2_stats")
        bn_step, bn_var, bn_root, bn_ready = sem("bn_step"), sem("bn_var"), sem("bn_root"), sem("bn_ready")
        bn_rows = sem("bn_rows")
        bn_shifted, bn_relu = sem("bn_shifted"), sem("bn_relu")
        l3_hot, l3_products, l3_scaled = sem("l3_hot"), sem("l3_products"), sem("l3_scaled")
        l3_map, l3_map_copied = sem("l3_map"), sem("l3_map_copied")

        early = [
            (IDX3[:, 0:CHUNKS], type_c),
            (w1[:, :], W1), (b1c[:, :], b1), (w2[:, :, :], W2.rearrange("(a p) c -> p a c", p=P)),
            (b2r, b2), (ub2r, ub2), (sb2r, sb2), (mb1r[:, H:2 * H], mb1), (sb1r, sb1),
            (wfn[:, 0:H], mW1[0:D, :]), (wfn[:, H:2 * H], mW1[D:2 * D, :]),
            (MIXW[WIN:P, 0, :], mW1[2 * D:2 * D + DE, :]), (MIXW[WIN:P, 1, :], mW1[2 * D:2 * D + DE, :]),
            (mw2T[:, :], mW2T), (mb2c[:, :], mb2), (u1[0:D, :], uW1[0:D, :]), (uw1b[:, :], uW1[D:2 * D, :]),
            (GROW[:, :], gamma.rearrange("h o -> o h").to_broadcast([P, H])),
            (ub1c[:, :], ub1), (uw2[:, :], uW2), (wl1[:, :], Wl1), (wr1[:, :], Wr1), (gam[:, :], gamma),
            (bet[:, :], beta), (wl2[:, :], Wl2), (wr2[:, :], Wr2), (wrel[:, :], Wrel),
        ]
        ALL_LOADED = 16 * (len(early) + 1)

        block = ctx.enter_context(nc.Block())

        def rows_of(tab, u):
            return tab[bass.ds(u * UNIT, UNIT), :].rearrange("(a p) c -> p a c", p=HALF)

        def within(at):
            return nc.s_assert_within(at, 0, N)

        def units_of_turn(eng, i):
            return [eng.value_load(DONE_I[0:1, bass.ds(i + k, 1)], min_val=0, max_val=UNITS) for k in range(2)]

        def stage_of_turn(eng, turn_units, node, h):
            lo, hi = turn_units
            with eng.If(hi > lo):
                node(nc.s_assert_within(lo, 0, UNITS - 1), h)
                if h == SLOTS - 1:
                    second = eng.snap(lo + 1)
                    with eng.If(hi > second):
                        units(eng, second, hi, node)

        def units(eng, lo, hi, node):
            with eng.Fori(lo, hi) as u:
                for h in range(SLOTS):
                    node(nc.s_assert_within(u, 0, UNITS - 1), h)

        def first_left(eng):
            return eng.value_load(DONE_I[0:1, TURNS:TURNS + 1], min_val=0, max_val=UNITS)

        STORE = [32, 16, 16, 32, 16]

        def all_stored(p):
            return STORE[p] * (UNITS + 1)

        def slot_gathered(p, i):
            return i * (16 * GROUP) + 16 * GROUP * (TURNS * p + 1)

        @block.sync
        def _(sp):
            for h in range(SLOTS):
                sp.dma_start(IDXB[:, h, :], src_c[:, h * GROUP:(h + 1) * GROUP]).then_inc(idx_staged[h], 16)
            sp.dma_start(DI, dst_c).then_inc(x_in, 16)
            sp.dma_start(SRC[:, 0:CHUNKS], src_c).then_inc(src_in, 16)
            sp.dma_start(AGG[0:D, 0:N], xT).then_inc(loaded, 16)
            sp.dma_start(T1, dst_r).then_inc(rows_in, 16)
            for tile, array in early:
                sp.dma_start(tile, array).then_inc(loaded, 16)
            sp.wait_ge(zero_ready, 1)
            sp.dma_start(near_tab[N:N + P, :], ZERO[:, 0:H]).then_inc(rows_out, 16)
            sp.dma_start(near_tab[N + P:NPAD, :], ZERO[0:NPAD - N - P, 0:H]).then_inc(rows_out, 16)
            sp.wait_ge(prep, ROWS_READY)
            sp.dma_start(dst_rows[0, 0:SUPERS * SUPER].rearrange("(p c) -> p c", p=P), DST16).then_inc(rows_out, 16)
            sp.dma_start(dst_rows[0, SUPERS * SUPER:].rearrange("(p c) -> p c", p=P),
                         ZERO[:, 0:GROUP].bitcast(I16)).then_inc(rows_out, 16)

            def stream(s, b):
                w0 = sp.value_load(FIRST_I[0:1, bass.ds(s, 1)], min_val=0, max_val=N)
                sp.dma_start(MIXT[WIN:P, b, :], efT[:, bass.ds(s * SUPER, SUPER)]).then_inc(ef_in[b], 16)
                sp.dma_start(DROW[:, b, :], dst_rows[:, bass.ds(s * SUPER, SUPER)].to_broadcast([WIN, SUPER]))\
                  .then_inc(ef_in[b], 16)
                sp.dma_start(MIXW[0:WIN, b, :], near_tab[bass.ds(w0, WIN), :]).then_inc(ef_in[b], 16)
                n = sp.value_load(WINS_I[0:1, bass.ds(s, 1)], min_val=1, max_val=P + 4)
                with sp.If(n > 1):
                    with sp.Fori(1, n) as it:
                        sp.reg_add(more, more, 1)
                        sp.wait_ge(more_done, sp.snap(more))
                        sp.dma_start(MOREW, near_tab[bass.ds(within(w0 + it * WIN), WIN), :])\
                          .then_inc(more_in, 16)
                    sp.wait_ge(more_done, sp.snap(sp.snap(more) + 1))
                    sp.sem_inc(sp_go, 1)

            more = sp.alloc_register("sp_more")
            sp.reg_mov(more, 0)
            sp.wait_ge(const_pool, 2)
            sp.wait_ge(src_in, 16)
            for p in range(LAYERS):
                numbers = IDX3 if p == 4 else SRC
                if p == 4:
                    sp.wait_ge(prep, TABLES_READY)
                for h in range(SLOTS if p else 0):
                    sp.wait_ge(gathered[h], 16 * GROUP * TURNS * p)
                    sp.wait_ge(idx_staged[h], 16 * (TURNS + 1) * p)
                    sp.dma_start(IDXB[:, h, :], numbers[:, h * GROUP:(h + 1) * GROUP]).then_inc(idx_staged[h], 16)
                if p == 1:
                    sp.wait_ge(rows_out, ROWS_OUT)
                    sp.wait_ge(prep, TABLES_READY)
                    sp.wait_ge(stored[0], all_stored(0))
                    stream(0, 0)
                    stream(1, 1)
                with sp.Fori(0, TURNS) as i:
                    for h in range(SLOTS):
                        sp.wait_ge(gathered[h], slot_gathered(p, i))
                        sp.sem_inc(sp_go, 1)
                        sp.dma_start(IDXB[:, h, :], numbers[:, bass.ds(i * (SLOTS * GROUP) + (SLOTS + h) * GROUP, GROUP)])\
                          .then_inc(idx_staged[h], 16)
                        if p == 1:
                            sp.wait_ge(pre_done, i * SLOTS + (h + 2))
                            sp.sem_inc(sp_go, 1)
                            stream(i * SLOTS + (h + 2), h % 2)
            for h in range(SLOTS):
                sp.wait_ge(idx_staged[h], 16 * (TURNS + 1) * LAYERS)
            sp.wait_ge(stored[4], all_stored(4))

        @block.gpsimd
        def _(pool):
            nc.gpsimd.memset(SRC[:, CHUNKS:], 0).then_inc(const_pool, 1)
            nc.gpsimd.memset(IDX3[:, CHUNKS:], 0).then_inc(const_pool, 1)
            nc.gpsimd.iota(IOTA[:, :], [[1, P]], base=0, channel_multiplier=0,
                           allow_small_or_imprecise_dtypes=True).then_inc(const_pool, 1)
            nc.gpsimd.iota(PIOTA[:, :], [[0, 1]], base=0, channel_multiplier=1,
                           allow_small_or_imprecise_dtypes=True).then_inc(const_pool, 1)

            def gathers(p, i, h):
                pool.wait_ge(idx_staged[h], i * 16 + 16 * ((TURNS + 1) * p + 1))
                pool.wait_ge(released, i * SLOTS + (SUPERS * p + h + 1))
                pool.sem_inc(pool_go, 1)
                for j in range(GROUP):
                    pool.indirect_dma_start(
                        out=G[:, h, j, 0:tabs[p].shape[1]], out_offset=None, in_=tabs[p],
                        in_offset=bass.IndirectOffsetOnAxis(ap=IDXB[:, h, j:j + 1], axis=0),
                    ).then_inc(gathered[h], 16)

            tabs = [x, far_tab, x2_tab, h_tab, rel_tab]
            for p in range(LAYERS):
                if p == 1:
                    pool.wait_ge(stored[0], all_stored(0))
                if p == 2:
                    pool.wait_ge(stored[1], all_stored(1))
                if p == 3:
                    pool.wait_ge(stored[2], all_stored(2))
                if p == 4:
                    pool.wait_ge(stored[3], all_stored(3))
                start = 0
                if p == 0:
                    for h in range(SLOTS):
                        gathers(0, 0, h)
                        if h == 0:
                            pool.wait_ge(prep, SPANS_READY)
                            nc.gpsimd.partition_all_reduce(MR, MM, P, RMAX).then_inc(spans_out, 1)
                    start = 1
                with pool.Fori(start, TURNS) as i:
                    for h in range(SLOTS):
                        gathers(p, i, h)
        @block.scalar
        def _(act):
            def root(p, u, n=1, k=0):
                act.wait_ge(var_ready[p], u * n + (k + 1))
                nc.scalar.activation(SQ[0:HALF, :], VE[0:HALF, :], ACT.Sqrt).then_inc(root_ready[p], 1)

            def flip_copy(p, u):
                m = D + 1 if p == 1 else D
                act.wait_ge(flipped[p], u + 1)
                nc.scalar.activation(XT[0:m, :], PT[0:m, :], ACT.Copy).then_inc(flip_copied[p], 1)

            def tile_free(p, u):
                act.wait_ge(stored[p], u * STORE[p] + STORE[p])
                act.sem_inc(act_go, 1)

            def node0(u, stage):
                if stage == 1:
                    act.wait_ge(l0_neg, u + 1)
                    for a in range(2):
                        last = nc.scalar.activation(POS[:, a * UNIT:(a + 1) * UNIT], NA[:, a * UNIT:(a + 1) * UNIT],
                                                    ACT.Relu, bias=b1c[:, a:a + 1])
                    last.then_inc(l0_pos, 1)
                    nc.scalar.activation(NEG[:, :], NEG[:, :], ACT.Exp).then_inc(l0_exp, 1)
                if stage == 2:
                    root(0, u)
                if stage == 3:
                    flip_copy(0, u)
                    tile_free(0, u)
                    act.wait_ge(l0_maps, u + 1)
                    nc.scalar.activation(STG[0:HALF, :, 0:2 * H], NA[0:HALF, :].rearrange("p (a c) -> p a c", a=2),
                                         ACT.Copy).then_inc(l0_maps_copied, 1)
                    act.wait_ge(l0_maps_copied, u + 1)
                    act.dma_start(rows_of(far_tab, u), STG[0:HALF, :, 0:H]).then_inc(stored[0], 16)
                    act.dma_start(rows_of(near_tab, u), STG[0:HALF, :, H:2 * H]).then_inc(stored[0], 16)

            def node1(u, stage):
                if stage == 1:
                    flip_copy(1, u)
                if stage == 2:
                    act.wait_ge(l1_hidden, u + 1)
                    nc.scalar.activation(POS[:, 0:UNIT], NA[:, 0:UNIT], ACT.Relu, bias=ub1c[:, 0:1])\
                        .then_inc(l1_relu, 1)
                if stage == 3:
                    root(1, u)
                    act.wait_ge(x_new[1], u + 1)
                    act.dma_start(rows_of(x2_tab, u), XS[0:HALF, :, :]).then_inc(stored[1], 16)

            def node2(u, stage):
                if stage == 1:
                    flip_copy(2, u)
                if stage == 2:
                    act.wait_ge(l2_products, u + 1)
                    for a in range(2):
                        last = nc.scalar.activation(Y2[0:HALF, a, :], NA[0:HALF, a * H:(a + 1) * H], ACT.Copy,
                                                    scale=IU[0:HALF, a:a + 1])
                    last.then_inc(l2_scaled, 1)
                    root(2, u)
                if stage == 3:
                    act.wait_ge(h_ready, u + 1)
                    act.dma_start(rows_of(h_tab, u), GH[0:HALF, :, :]).then_inc(stored[2], 16)
                    act.wait_ge(l2_flipped, u + 1)
                    act.sem_inc(act_go, 1)
                    nc.scalar.activation(HT[:, bass.ds(u * UNIT, UNIT)], NA[:, 0:UNIT], ACT.Copy).then_inc(l2_kept, 1)

            def node3(u, stage):
                if stage == 0:
                    nc.scalar.activation(HB, HT[:, bass.ds(u * UNIT, UNIT)], ACT.Relu,
                                         bias=BSH[:, 0:1], scale=BSC[:, 0:1]).then_inc(l3_hot, 1)
                if stage == 1:
                    act.wait_ge(l3_products, u + 1)
                    for a in range(2):
                        last = nc.scalar.activation(Y2[0:HALF, a, 0:D], NB[0:HALF, a * D:(a + 1) * D], ACT.Copy,
                                                    scale=IU[0:HALF, a:a + 1])
                    last.then_inc(l3_scaled, 1)
                    root(3, u, 3, 0)
                if stage == 2:
                    for k in (1, 2):
                        root(3, u, 3, k)
                if stage == 3:
                    flip_copy(3, u)
                    tile_free(3, u)
                    for a in range(2):
                        for k in (2 * a, 2 * a + 1):
                            c = slice(k % 2 * 512, k % 2 * 512 + 512)
                            act.wait_ge(l3_map, u * 4 + (k + 1))
                            nc.scalar.activation(STG[0:HALF, a, c], PH[a][0:HALF, c], ACT.Copy)\
                                .then_inc(l3_map_copied, 1)
                        act.wait_ge(l3_map_copied, u * 4 + (2 * a + 2))
                        act.dma_start(rel_tab[bass.ds(u * (UNIT * R) + a * (HALF * R), HALF * R), :]
                                      .rearrange("(p r) d -> p (r d)", r=R), STG[0:HALF, a, :]).then_inc(stored[3], 16)

            def node4(u, stage):
                if stage == 2:
                    root(4, u)
                if stage == 3:
                    act.wait_ge(x_new[4], u + 1)
                    act.dma_start(rows_of(out, u), XS[0:HALF, :, :]).then_inc(stored[4], 16)

            def batch_norm_root():
                act.wait_ge(bn_var, 1)
                nc.scalar.activation(BT[:, 1:2], BT[:, 0:1], ACT.Sqrt).then_inc(bn_root, 1)

            node = [node0, node1, node2, node3, node4]
            for p in range(LAYERS):
                act.sem_inc(stored[p], STORE[p])
            act.wait_ge(zero_ready, 1)
            nc.scalar.copy(AGG[D:P, 0:N].rearrange("p (u n) -> p u n", n=UNIT),
                           ZERO[D:P, :].unsqueeze(1).to_broadcast([P - D, UNITS, UNIT])).then_inc(agg_zero, 1)
            nc.scalar.copy(AGG[:, N:NPAD], ZERO[:, 0:NPAD - N]).then_inc(agg_zero, 1)
            act.wait_ge(loaded, ALL_LOADED)
            act.dma_start(X[0:HALF, :, 0:D], x.rearrange("(a p) c -> p a c", p=HALF)).then_inc(x_loaded, 16)
            act.wait_ge(prep, TABLES_READY)
            act.sem_inc(act_go, 1)
            for p in range(LAYERS):
                if p == 2:
                    act.wait_ge(ef_in[1], 48 * (SUPERS // 2 + 1))
                if p == 3:
                    act.wait_ge(bn_ready, 1)
                    act.wait_ge(stored[2], all_stored(2))
                with act.Fori(0, TURNS) as i:
                    turn_units = units_of_turn(act, i)
                    for h in range(SLOTS):
                        if p == 1:
                            act.wait_ge(mixed, i * SLOTS + (h + 2))
                            nc.scalar.activation(HID[:, h % 2, :], HID[:, h % 2, :], ACT.Relu).then_inc(relu_done, 1)
                        if p == 3:
                            act.wait_ge(bn_shifted, i * SLOTS + (h + 1))
                            nc.scalar.activation(G[:, h, :, :], G[:, h, :, :], ACT.Relu).then_inc(bn_relu, 1)
                        stage_of_turn(act, turn_units, node[p], h)
                left = first_left(act)
                units(act, left, UNITS, node[p])
                if p == 2:
                    batch_norm_root()

        @block.vector
        def _(dve):
            step = [0]

            def link(ins):
                step[0] += 1
                ins.then_inc(prep, 1)
                dve.wait_ge(prep, step[0])

            nc.vector.memset(ONES[:, :], 1.0)
            nc.vector.memset(rows[:, 3 * D:3 * D + H], 0.0)
            nc.vector.memset(G[:, :, :, D:D + 1], 1.0).then_inc(released, SLOTS)
            nc.vector.memset(ZERO[:, :], 0.0).then_inc(zero_ready, 1)
            dve.wait_ge(x_in, 16)
            link(nc.vector.tensor_copy(DF, DI))
            DFv = DF.rearrange("p (s j) -> p s j", j=GROUP)
            link(nc.vector.tensor_reduce(MM[:, 0:SUPERS], DFv, AX.X, ALU.max))
            link(nc.vector.tensor_reduce(MR[:, 0:SUPERS], DFv, AX.X, ALU.min))
            link(nc.vector.tensor_scalar_mul(MM[:, SUPERS:], MR[:, 0:SUPERS], -1.0))
            link(nc.vector.memset(FIRST[:, SUPERS:], 0.0))
            assert step[0] == SPANS_READY
            dve.wait_ge(const_pool, 4)
            link(nc.vector.tensor_scalar(IDENT[:, :], IOTA[:, :], PIOTA[:, 0:1], None, ALU.is_equal))
            dve.wait_ge(spans_out, 1)
            link(nc.vector.memset(WINS_I[:, SUPERS:], 1))
            link(nc.vector.tensor_scalar_mul(FIRST[:, 0:SUPERS], MR[:, SUPERS:], -1.0))
            link(nc.vector.tensor_scalar(FIRSTP[:, :], FIRST[:, :], PIOTA[:, 0:1], None, ALU.add))
            link(nc.vector.tensor_copy(FIRST_I[:, :], FIRST[0:1, :]))
            link(nc.vector.tensor_tensor(DREL[:, 0:SUPERS, :], DFv,
                                         FIRST[:, 0:SUPERS].unsqueeze(2).to_broadcast([P, SUPERS, GROUP]),
                                         ALU.subtract))
            link(nc.vector.tensor_copy(DREL[:, SUPERS, :], DREL[:, 0, :]))
            assert WIN == 3 * 32 and N // 32 < 512
            link(nc.vector.tensor_tensor(FA[:, 0, 0:SUPERS], MR[0:1, 0:SUPERS], FIRST[0:1, 0:SUPERS], ALU.subtract))
            wins = WINS_I[:, 0:SUPERS]
            link(nc.vector.tensor_copy(wins, FA[:, 0, 0:SUPERS]))
            link(nc.vector.tensor_single_scalar(wins, wins, 5, ALU.logical_shift_right))
            link(nc.vector.tensor_scalar(wins, wins, 171.0, None, ALU.mult))
            link(nc.vector.tensor_single_scalar(wins, wins, 9, ALU.logical_shift_right))
            link(nc.vector.tensor_scalar(wins, wins, 1.0, None, ALU.add))
            link(nc.vector.memset(FA[:, :, :], float(N)))
            link(nc.vector.tensor_reduce(FA[:, 0, 0:TURNS], FIRST[0:1, 0:SUPERS].rearrange("p (i h) -> p i h", h=SLOTS),
                                         AX.X, ALU.min))
            a = 0
            for k in (1, 2, 4, 8, 16, 32):
                link(nc.vector.tensor_tensor(FA[:, 1 - a, 0:TURNS], FA[:, a, 0:TURNS], FA[:, a, k:k + TURNS], ALU.min))
                a = 1 - a
            link(nc.vector.tensor_scalar(FA[:, 1 - a, 0:TURNS], FA[:, a, 0:TURNS], -(UNIT - 1) / 2, 1.0 / UNIT,
                                         ALU.add, ALU.mult))
            link(nc.vector.tensor_scalar_max(FA[:, a, 0:TURNS], FA[:, 1 - a, 0:TURNS], 0.0))
            link(nc.vector.tensor_copy(DONE_I[:, 1:], FA[:, a, 0:TURNS]))
            link(nc.vector.memset(DONE_I[:, 0:2], 0))
            dve.wait_ge(rows_in, 16)
            link(nc.vector.tensor_copy(DST16, T1))
            assert step[0] == ROWS_READY, step[0]
            dve.wait_ge(products, 1)
            link(nc.vector.tensor_copy(mu[:, :], NA[:, 0:H]))
            link(nc.vector.tensor_copy(u1[D:D + 1, :], NB[0:1, 0:H]))
            dve.wait_ge(agg_zero, 2)
            dve.sem_inc(mixed, 1)
            dve.sem_inc(added, 2)
            assert step[0] == PREP_READY, step[0]

            def one_hot(b, d):
                return nc.vector.tensor_tensor(OH[:, b, :, :], IOTA[:, 0:WIN].unsqueeze(1).to_broadcast([P, GROUP, WIN]),
                                               d.unsqueeze(2).to_broadcast([P, GROUP, WIN]), ALU.is_equal)

            def targets(s):
                return DREL[:, bass.ds(s, 1), :].rearrange("p a j -> p (a j)")

            one_hot(0, targets(0)).then_inc(onehot_ready, 1)
            dve.wait_ge(src_in, 16)
            dve.wait_ge(loaded, ALL_LOADED)
            link(nc.vector.tensor_scalar(DI, SRC[:, 0:CHUNKS], float(R), None, ALU.mult))
            link(nc.vector.tensor_tensor(IDX3[:, 0:CHUNKS], IDX3[:, 0:CHUNKS], DI, ALU.add))
            assert step[0] == TABLES_READY, step[0]

            far = dve.alloc_register("dve_far")
            steps = dve.alloc_register("dve_steps")
            more = dve.alloc_register("dve_more")
            for reg in (far, steps, more):
                dve.reg_mov(reg, 0)

            def far_link(ins):
                ins.then_inc(far_step, 1)
                dve.reg_add(steps, steps, 1)
                dve.wait_ge(far_step, dve.snap(steps))
                dve.sem_inc(dve_go, 1)

            def add_window(b, m, at):
                dst = AGG[0:m, bass.ds(at, WIN)]
                return nc.vector.tensor_tensor(dst, dst, PAG[b][0:m, 0:WIN], ALU.add)

            def add_super(p, s, h, m):
                b = h % 2
                w0 = dve.value_load(FIRST_I[0:1, bass.ds(s, 1)], min_val=0, max_val=N)
                n = dve.value_load(WINS_I[0:1, bass.ds(s, 1)], min_val=1, max_val=P + 4)
                dve.wait_ge(summed, s + (SUPERS * p + 1))
                dve.wait_ge(added, s + (SUPERS * p + 2))
                add_window(b, m, w0).then_inc(added, 1)
                with dve.If(n > 1):
                    dve.wait_ge(added, s + (SUPERS * p + 3))
                    far_link(nc.vector.tensor_scalar(DCUR[:, :], targets(s), 0.0, None, ALU.add))
                    with dve.Fori(1, n) as it:
                        far_link(nc.vector.tensor_scalar(DCUR[:, :], DCUR[:, :], -float(WIN), None, ALU.add))
                        one_hot(b, DCUR[:, :]).then_inc(far_hot, 1)
                        dve.reg_add(far, far, 1)
                        dve.wait_ge(far_summed, dve.snap(far))
                        far_link(add_window(b, m, within(w0 + it * WIN)))
                if p != 1:
                    release(h)

            def release(h):
                nc.vector.memset(TICK[:, h:h + 1], 0.0).then_inc(released, 1)

            def hot_T(t, b, uses, first=False):
                dve.wait_ge(ef_in[b], uses * 48)
                if not first:
                    dve.wait_ge(pre_done, t)
                dve.sem_inc(dve_go, 1)
                nc.vector.tensor_scalar(MIXT[0:WIN, b, :], DROW[:, b, :], FIRSTP[0:WIN, bass.ds(t, 1)], None,
                                        ALU.is_equal).then_inc(hotT_ready, 1)

            def more_hot_T(t, b):
                n = dve.value_load(WINS_I[0:1, bass.ds(t, 1)], min_val=1, max_val=P + 4)
                with dve.If(n > 1):
                    dve.wait_ge(pre_done, t + 2)
                    far_link(nc.vector.tensor_scalar(FCUR[:, :], FIRSTP[:, bass.ds(t, 1)], 0.0, None, ALU.add))
                    with dve.Fori(1, n) as it:
                        dve.reg_add(more, more, 1)
                        dve.wait_ge(more_done, dve.snap(more))
                        far_link(nc.vector.tensor_scalar(FCUR[:, :], FCUR[:, :], float(WIN), None, ALU.add))
                        nc.vector.tensor_scalar(MIXT[0:WIN, b, :], DROW[:, b, :], FCUR[0:WIN, 0:1], None,
                                                ALU.is_equal).then_inc(more_hot, 1)
                    dve.wait_ge(more_done, dve.snap(dve.snap(more) + 1))
                    dve.sem_inc(dve_go, 1)

            def move(dst, src_):
                return nc.vector.tensor_scalar(dst, src_, 1.0, None, ALU.mult)

            def steps_of(p, u, before=0):
                count = [before]

                def run(*instructions):
                    count[0] += 1
                    instructions[-1].then_inc(chain[p], 1)
                    dve.wait_ge(chain[p], u * CHAIN[p] + count[0])

                def done():
                    assert count[0] == CHAIN[p], (p, count[0])
                return run, done

            def fetch(p, u, m):
                move(Z[0:m, :], AGG[0:m, bass.ds(u * UNIT, UNIT)])
                if p in (2, 3):
                    move(IU[0:HALF, :], INV[0:HALF, bass.ds(u * 2, 2)])
                last = move(XU[0:HALF, :, :] if p else XU[0:HALF, :, 0:D],
                            X[0:HALF, bass.ds(u * 2, 2), :] if p else X[0:HALF, bass.ds(u * 2, 2), 0:D])
                last.then_inc(staged[p], 1)
                dve.wait_ge(staged[p], u + 1)
                nc.vector.tensor_scalar(AGG[:, bass.ds(u * UNIT, UNIT)], ZERO[:, :], 0.0, None, ALU.add)\
                  .then_inc(cleared[p], 1)

            def layer_norm(p, u, run, n=1, k=0):
                run(nc.vector.bn_stats(ST6[0:HALF, 0, :], Y[0:HALF, 0, 0:D]),
                    nc.vector.bn_stats(ST6[0:HALF, 1, :], Y[0:HALF, 1, 0:D]))
                dve.sem_inc(dve_go, 1)
                run(nc.vector.bn_aggr(MV[0:HALF, 0, :], ST6[0:HALF, 0, :]),
                    nc.vector.bn_aggr(MV[0:HALF, 1, :], ST6[0:HALF, 1, :]))
                nc.vector.tensor_scalar(VE[0:HALF, :], MV[0:HALF, :, 1], LN_EPS, None, ALU.add).then_inc(var_ready[p], 1)
                dve.wait_ge(root_ready[p], u * n + (k + 1))
                run(nc.vector.reciprocal(RS[0:HALF, :], SQ[0:HALF, :]))
                if p in (1, 4):
                    dve.wait_ge(stored[p], u * STORE[p] + STORE[p])
                for a_ in range(2):
                    last = nc.vector.tensor_scalar(XS[0:HALF, a_, :], Y[0:HALF, a_, 0:D], MV[0:HALF, a_, 0:1],
                                                   RS[0:HALF, a_:a_ + 1], ALU.subtract, ALU.mult)
                last.then_inc(x_new[p], 1)
                if p < 4:
                    dve.wait_ge(x_new[p], u + 1)
                    move(X[0:HALF, bass.ds(u * 2, 2), 0:D], XS[0:HALF, :, :]).then_inc(x_kept[p], 1)

            def inverse_norm(p, u, run, w, n, k):
                y = Y[0:HALF, :, 0:w]
                run(nc.vector.tensor_tensor(Y2[0:HALF, :, 0:w], y, y, ALU.mult))
                run(nc.vector.tensor_reduce(SS[0:HALF, :], Y2[0:HALF, :, 0:w], AX.X, ALU.add))
                nc.vector.tensor_scalar(VE[0:HALF, :], SS[0:HALF, :], NORM_FLOOR_SQ, None, ALU.max)\
                  .then_inc(var_ready[p], 1)
                dve.wait_ge(root_ready[p], u * n + (k + 1))
                run(nc.vector.reciprocal(RS[0:HALF, :], SQ[0:HALF, :]))

            def halves(t, w=D):
                return t.rearrange("p (a c) -> p a c", c=w)

            def node0(u, stage):
                if stage == 0:
                    dve.wait_ge(x_loaded, 16)
                    fetch(0, u, D + 1)
                if stage == 1:
                    run, done = steps_of(0, u)
                    dve.wait_ge(l0_hidden, u + 1)
                    for a_ in range(2):
                        last = nc.vector.tensor_scalar(NEG[:, a_ * UNIT:(a_ + 1) * UNIT],
                                                       NA[:, a_ * UNIT:(a_ + 1) * UNIT],
                                                       b1c[:, a_:a_ + 1], 0.0, ALU.add, ALU.min)
                    last.then_inc(l0_neg, 1)
                    degree = NB[0:HALF, 508:510]
                    move(X[0:HALF, bass.ds(u * 2, 2), D], degree)
                    run(nc.vector.tensor_scalar(IU[0:HALF, :], degree, 1.0, None, ALU.max))
                    run(nc.vector.reciprocal(SS[0:HALF, :], IU[0:HALF, :]))
                    move(INV[0:HALF, bass.ds(u * 2, 2)], SS[0:HALF, :])
                    dve.wait_ge(l0_pos, u + 1)
                    dve.wait_ge(l0_exp, u + 1)
                    nc.vector.scalar_tensor_tensor(NEG[:, :], NEG[:, :], -1.0, POS[:, :], ALU.add, ALU.add)\
                      .then_inc(l0_elu, 1)
                if stage == 2:
                    run, done = steps_of(0, u, 2)
                    dve.wait_ge(y_ready[0], u + 1)
                    run(nc.vector.tensor_tensor(Y[0:HALF, :, 0:D], halves(NB[0:HALF, 0:2 * D]), XU[0:HALF, :, 0:D],
                                                ALU.add))
                    layer_norm(0, u, run)
                    done()

            def node1(u, stage):
                if stage == 0:
                    fetch(1, u, H)
                if stage == 3:
                    run, done = steps_of(1, u)
                    dve.wait_ge(y_ready[1], u + 1)
                    run(nc.vector.tensor_tensor(Y[0:HALF, :, 0:D], halves(NB[0:HALF, 0:2 * D]), XU[0:HALF, :, 0:D],
                                                ALU.add))
                    layer_norm(1, u, run)
                    done()

            def node2(u, stage):
                if stage == 0:
                    fetch(2, u, D)
                if stage == 2:
                    run, done = steps_of(2, u)
                    dve.wait_ge(l2_scaled, u + 1)
                    run(nc.vector.tensor_tensor(Y[0:HALF, :, :], halves(NB[0:HALF, 0:2 * H], H), Y2[0:HALF, :, :],
                                                ALU.add))
                    inverse_norm(2, u, run, H, 1, 0)
                    for a_ in range(2):
                        last = nc.vector.tensor_scalar(Y2[0:HALF, a_, :], Y[0:HALF, a_, :], RS[0:HALF, a_:a_ + 1],
                                                       None, ALU.mult)
                    last.then_inc(l2_normed, 1)
                    dve.wait_ge(l2_normed, u + 1)
                    dve.wait_ge(stored[2], u * STORE[2] + STORE[2])
                    nc.vector.tensor_tensor(GH[0:HALF, :, :], Y2[0:HALF, :, :],
                                            GROW[0:HALF, :].unsqueeze(1).to_broadcast([HALF, 2, H]), ALU.mult)\
                      .then_inc(h_ready, 1)
                    done()
                if stage == 3:
                    dve.wait_ge(l2_kept, u + 1)
                    dve.sem_inc(dve_go, 1)
                    nc.vector.bn_stats(BST[:, bass.ds(u, 1), :].rearrange("p a c -> p (a c)"), NA[:, 0:UNIT])\
                      .then_inc(l2_stats, 1)

            def batch_norm():
                dve.wait_ge(l2_stats, UNITS)
                nc.vector.bn_aggr(BMV[:, :], BST[:, :, :].rearrange("p u c -> p (u c)")).then_inc(bn_step, 1)
                dve.wait_ge(bn_step, 1)
                nc.vector.tensor_scalar(BT[:, 0:1], BMV[:, 1:2], BN_EPS, None, ALU.add).then_inc(bn_var, 1)
                dve.wait_ge(bn_root, 1)
                nc.vector.reciprocal(BT[:, 2:3], BT[:, 1:2]).then_inc(bn_step, 1)
                dve.wait_ge(bn_step, 2)
                nc.vector.tensor_tensor(BSC[:, :], BT[:, 2:3], gam[:, :], ALU.mult).then_inc(bn_step, 1)
                dve.wait_ge(bn_step, 3)
                nc.vector.tensor_tensor(BT[:, 3:4], BMV[:, 0:1], BSC[:, :], ALU.mult).then_inc(bn_step, 1)
                nc.vector.tensor_tensor(BC[:, 0:1], BMV[:, 0:1], gam[:, :], ALU.mult).then_inc(bn_step, 1)
                nc.vector.tensor_tensor(BC[:, 1:2], BT[:, 1:2], bet[:, :], ALU.mult).then_inc(bn_step, 1)
                dve.wait_ge(bn_step, 6)
                nc.vector.tensor_tensor(BC[:, 2:3], BC[:, 1:2], BC[:, 0:1], ALU.subtract).then_inc(bn_step, 1)
                nc.vector.tensor_scalar(wl2[:, :], wl2[:, :], BT[:, 2:3], None, ALU.mult).then_inc(bn_step, 1)
                nc.vector.tensor_tensor(BSH[:, :], bet[:, :], BT[:, 3:4], ALU.subtract).then_inc(bn_ready, 1)

                dve.wait_ge(bn_rows, 1)
                move(CROW[:, :], NA[:, 0:H]).then_inc(bn_step, 1)
                dve.wait_ge(bn_step, 9)

            def shift(p, i, h):
                rows_ = G[:, h, :, :]
                dve.wait_ge(gathered[h], slot_gathered(p, i))
                nc.vector.tensor_tensor(rows_, rows_, CROW[:, :].unsqueeze(1).to_broadcast([P, GROUP, H]), ALU.add)\
                  .then_inc(bn_shifted, 1)

            def node3(u, stage):
                def add_normed(run, k):
                    inverse_norm(3, u, run, D, 3, k)
                    run(*[nc.vector.scalar_tensor_tensor(Y[0:HALF, a_, 0:D], Y[0:HALF, a_, 0:D], RS[0:HALF, a_:a_ + 1],
                                                         XU[0:HALF, a_, 0:D], ALU.mult, ALU.add) for a_ in range(2)])

                if stage == 0:
                    fetch(3, u, H)
                if stage == 1:
                    run, done = steps_of(3, u)
                    dve.wait_ge(l3_scaled, u + 1)
                    run(nc.vector.tensor_tensor(Y[0:HALF, :, 0:D], halves(NA[0:HALF, 0:2 * D]), Y2[0:HALF, :, 0:D],
                                                ALU.add))
                    add_normed(run, 0)
                    dve.sem_inc(dve_go, 1)
                if stage == 2:
                    run, done = steps_of(3, u, 5)
                    add_normed(run, 1)
                    layer_norm(3, u, run, 3, 2)
                    done()

            def node4(u, stage):
                if stage == 0:
                    fetch(4, u, D)
                if stage == 2:
                    run, done = steps_of(4, u)
                    dve.wait_ge(y_ready[4], u + 1)
                    run(nc.vector.tensor_tensor(Y[0:HALF, :, 0:D], halves(NB[0:HALF, 0:2 * D]), XU[0:HALF, :, 0:D],
                                                ALU.add))
                    layer_norm(4, u, run)
                    done()

            node = [node0, node1, node2, node3, node4]
            for p in range(LAYERS):
                m = (D + 1, H, D, H, D)[p]
                if p:
                    dve.wait_ge(cleared[p - 1], UNITS)
                    if p != 3:
                        dve.wait_ge(x_kept[p - 1], UNITS)
                    dve.sem_inc(dve_go, 1)
                if p == 1:
                    hot_T(0, 0, 1, first=True)
                    more_hot_T(0, 0)
                with dve.Fori(0, TURNS) as i:
                    turn_units = units_of_turn(dve, i)
                    for h in range(SLOTS):
                        if p == 1:
                            hot_T(i * SLOTS + (h + 1), (h + 1) % 2, i * (SLOTS // 2) + ((h + 1) // 2 + 1))
                            dve.wait_ge(pre_done, i * SLOTS + (h + 2))
                            dve.wait_ge(gathered[h], slot_gathered(p, i))
                            nc.vector.tensor_tensor(HID[:, h % 2, :], PH[h % 2][:, :],
                                                    G[:, h, :, :].rearrange("p j c -> p (j c)"), ALU.add)\
                              .then_inc(mixed, 1)
                            release(h)
                        if p == 3:
                            shift(p, i, h)
                        if h:
                            add_super(p, i * SLOTS + (h - 1), h - 1, m)
                        else:
                            with dve.If(i > 0):
                                add_super(p, nc.s_assert_within(i * SLOTS - 1, 0, SUPERS - 1), SLOTS - 1, m)
                        one_hot((h + 1) % 2, targets(i * SLOTS + (h + 1))).then_inc(onehot_ready, 1)
                        if p == 1:
                            more_hot_T(i * SLOTS + (h + 1), (h + 1) % 2)
                        if h == 0:
                            dve.wait_ge(added, i * SLOTS + (SUPERS * p + 2))
                            dve.sem_inc(dve_go, 1)
                        stage_of_turn(dve, turn_units, node[p], h)
                left = first_left(dve)
                add_super(p, SUPERS - 1, SLOTS - 1, m)
                dve.wait_ge(added, SUPERS * (p + 1) + 2)
                units(dve, left, UNITS, node[p])
                if p == 2:
                    batch_norm()

        @block.tensor
        def _(pe):
            def mm(dst, lhsT, rhs, start=True, stop=True):
                return nc.tensor.matmul(dst, lhsT, rhs, start=start, stop=stop, skip_group_check=True)

            def with_bias(dst, lhsT, rhs, bias):
                mm(dst, lhsT, rhs, stop=False)
                return mm(dst, ONES[0:1, 0:HALF], bias, start=False)

            def half(a):
                return slice(a * HALF, (a + 1) * HALF)

            pe.sem_inc(more_done, 1)
            pe.sem_inc(pre_done, 1)
            pe.wait_ge(loaded, ALL_LOADED)
            mm(NA[:, 0:H], mw2T[:, :], uw1b[:, :])
            mm(NB[0:1, 0:H], mb2c[:, :], uw1b[:, :]).then_inc(products, 1)
            pe.wait_ge(prep, PREP_READY)
            pe.sem_inc(pe_go, 1)
            far = pe.alloc_register("pe_far")
            more = pe.alloc_register("pe_more")
            for reg in (far, more):
                pe.reg_mov(reg, 0)

            def sum_window(p, h, m):
                msg = HID[:, h % 2, :].rearrange("p (j c) -> p j c", j=GROUP) if p == 1 else G[:, h, :, :]
                for j in range(GROUP):
                    last = mm(PAG[h % 2][0:m, 0:WIN], msg[:, j, 0:m], OH[:, h % 2, j, :], j == 0, j == GROUP - 1)
                return last

            def sum_super(p, i, h, n, m):
                pe.wait_ge(onehot_ready, i * SLOTS + (SUPERS * p + h + 1))
                pe.wait_ge(added, i * SLOTS + (SUPERS * p + h + 1))
                if p == 1:
                    pe.wait_ge(relu_done, i * SLOTS + (h + 1))
                elif p == 3:
                    pe.wait_ge(bn_relu, i * SLOTS + (h + 1))
                else:
                    pe.wait_ge(gathered[h], i * (16 * GROUP) + 16 * GROUP * (TURNS * p + 1))
                sum_window(p, h, m).then_inc(summed, 1)
                with pe.If(n > 1):
                    with pe.Fori(1, n) as it:
                        pe.reg_add(far, far, 1)
                        pe.wait_ge(far_hot, pe.snap(far))
                        sum_window(p, h, m).then_inc(far_summed, 1)

            def pre(t, b, uses, first=False):
                n = pe.value_load(WINS_I[0:1, bass.ds(t, 1)], min_val=1, max_val=P + 4)
                pe.wait_ge(ef_in[b], uses * 48)
                pe.wait_ge(hotT_ready, t + 1)
                if not first:
                    pe.wait_ge(mixed, t)
                pe.sem_inc(pe_go, 1)
                for j in range(GROUP):
                    c = slice(j * P, (j + 1) * P)
                    last = mm(PH[b][:, c], MIXT[:, b, c], MIXW[:, b, :], j % 4 == 0, j % 4 == 3)
                last.then_inc(pre_done, 1)
                with pe.If(n > 1):
                    with pe.Fori(1, n) as it:
                        pe.reg_add(more, more, 1)
                        window = pe.snap(more)
                        landed = pe.snap(window * 16)
                        pe.wait_ge(more_in, landed)
                        pe.wait_ge(more_hot, window)
                        for j in range(GROUP):
                            c = slice(j * P, (j + 1) * P)
                            last = mm(PH[b][:, c], MIXT[0:WIN, b, c], MOREW, False, j % 4 == 3)
                        last.then_inc(more_done, 1)

            def flip(p, tile, m):
                for a in range(2):
                    last = mm(PT[0:m, half(a)], tile[0:HALF, a, 0:m], IDENT[0:HALF, 0:HALF])
                last.then_inc(flipped[p], 1)

            def node0(u, stage):
                if stage == 1:
                    pe.wait_ge(staged[0], u + 1)
                    for a in range(2):
                        mm(NA[:, a * UNIT:(a + 1) * UNIT], w1[:, a * H:(a + 1) * H], Z[0:D, :])
                        last = mm(NB[0:HALF, 508 + a:509 + a], Z[D:D + 1, half(a)], ONES[D:D + 1, 0:1])
                    last.then_inc(l0_hidden, 1)
                if stage == 2:
                    pe.wait_ge(l0_elu, u + 1)
                    for a in range(2):
                        dst = NB[0:HALF, a * D:(a + 1) * D]
                        mm(dst, NEG[:, half(a)], w2[:, 0, :], stop=False)
                        mm(dst, NEG[:, UNIT + a * HALF:UNIT + (a + 1) * HALF], w2[:, 1, :], False, False)
                        last = mm(dst, ONES[0:1, 0:HALF], b2r, False)
                    last.then_inc(y_ready[0], 1)
                if stage == 3:
                    pe.wait_ge(x_new[0], u + 1)
                    flip(0, XS, D)
                    pe.wait_ge(flip_copied[0], u + 1)
                    for a in range(2):
                        last = with_bias(NA[0:HALF, a * 2 * H:(a + 1) * 2 * H], XT[0:D, half(a)], wfn[:, :], mb1r)
                    last.then_inc(l0_maps, 1)
                    pe.wait_ge(l0_maps_copied, u + 1)
                    pe.sem_inc(pe_go, 1)

            def node1(u, stage):
                if stage == 1:
                    pe.wait_ge(staged[1], u + 1)
                    flip(1, XU, D + 1)
                if stage == 2:
                    pe.wait_ge(flip_copied[1], u + 1)
                    mm(NA[:, 0:UNIT], u1[:, :], XT[:, :], stop=False)
                    mm(NA[:, 0:UNIT], mu[:, :], Z[:, :], False).then_inc(l1_hidden, 1)
                if stage == 3:
                    pe.wait_ge(l1_relu, u + 1)
                    for a in range(2):
                        last = with_bias(NB[0:HALF, a * D:(a + 1) * D], POS[:, half(a)], uw2[:, :], ub2r)
                    last.then_inc(y_ready[1], 1)

            def node2(u, stage):
                if stage == 1:
                    pe.wait_ge(staged[2], u + 1)
                    flip(2, XU, D)
                if stage == 2:
                    pe.wait_ge(flip_copied[2], u + 1)
                    for a in range(2):
                        mm(NA[0:HALF, a * H:(a + 1) * H], Z[0:D, half(a)], wl1[:, :])
                        last = with_bias(NB[0:HALF, a * H:(a + 1) * H], XT[0:D, half(a)], wr1[:, :], sb1r)
                    last.then_inc(l2_products, 1)
                if stage == 3:
                    pe.wait_ge(l2_normed, u + 1)
                    for a in range(2):
                        last = mm(NA[:, half(a)], Y2[0:HALF, a, :], IDENT[0:HALF, 0:HALF])
                    last.then_inc(l2_flipped, 1)

            def batch_norm_row():
                pe.wait_ge(bn_ready, 1)
                mm(NA[:, 0:H], BC[:, 2:3].to_broadcast([P, P]), IDENT[:, :]).then_inc(bn_rows, 1)

            def node3(u, stage):
                if stage == 1:
                    pe.wait_ge(staged[3], u + 1)
                    pe.wait_ge(l3_hot, u + 1)
                    for a in range(2):
                        mm(NB[0:HALF, a * D:(a + 1) * D], Z[:, half(a)], wl2[:, :])
                        last = with_bias(NA[0:HALF, a * D:(a + 1) * D], HB[:, half(a)], wr2[:, :], sb2r)
                    last.then_inc(l3_products, 1)
                if stage == 3:
                    pe.wait_ge(x_new[3], u + 1)
                    flip(3, XS, D)
                    pe.wait_ge(flip_copied[3], u + 1)
                    for k in range(4):
                        c = slice(k % 2 * 512, k % 2 * 512 + 512)
                        mm(PH[k // 2][0:HALF, c], XT[0:D, half(k // 2)], wrel[:, c]).then_inc(l3_map, 1)

            def node4(u, stage):
                if stage == 1:
                    pe.wait_ge(staged[4], u + 1)
                    for a in range(2):
                        last = mm(NB[0:HALF, a * D:(a + 1) * D], Z[0:D, half(a)], IDENT[0:D, 0:D])
                    last.then_inc(y_ready[4], 1)

            node = [node0, node1, node2, node3, node4]
            for p in range(LAYERS):
                m = (D + 1, H, D, H, D)[p]
                if p == 1:
                    pre(0, 0, 1, first=True)
                with pe.Fori(0, TURNS) as i:
                    turn_units = units_of_turn(pe, i)
                    for h in range(SLOTS):
                        n = pe.value_load(WINS_I[0:1, bass.ds(i * SLOTS + h, 1)], min_val=1, max_val=P + 4)
                        if p == 1:
                            pre(i * SLOTS + (h + 1), (h + 1) % 2, i * (SLOTS // 2) + ((h + 1) // 2 + 1))
                        stage_of_turn(pe, turn_units, node[p], h)
                        sum_super(p, i, h, n, m)
                left = first_left(pe)
                units(pe, left, UNITS, node[p])
                if p == 2:
                    batch_norm_row()


def kernel(x, src, dst, edge_attr_32, edge_type_16, L0_gnn_W1, L0_gnn_b1, L0_gnn_W2, L0_gnn_b2,
           L1_gnn_mW1, L1_gnn_mb1, L1_gnn_mW2, L1_gnn_mb2, L1_gnn_uW1, L1_gnn_ub1, L1_gnn_uW2, L1_gnn_ub2,
           L2_gnn_Wl1, L2_gnn_Wr1, L2_gnn_b1, L2_gnn_gamma1, L2_gnn_beta1, L2_gnn_Wl2, L2_gnn_Wr2, L2_gnn_b2,
           L3_gnn_weight):
    import numpy as np
    import concourse.bacc as bacc
    from concourse.bass_utils import run_bass_kernel_spmd

    def padded(a, last, fill):
        a = np.asarray(a)
        out = np.full(a.shape[:-1] + (last,), fill, a.dtype)
        out[..., :a.shape[-1]] = a
        return out

    def by_chunk(a, fill):
        return padded(a, CHUNKS * P, fill).reshape(CHUNKS, P).T

    def column(a):
        return np.asarray(a).reshape(-1, 1)

    def row(a):
        return np.asarray(a).reshape(1, -1)

    arrays = {
        "x": x, "xT": np.asarray(x).T,
        "src_c": by_chunk(src, 0), "dst_c": by_chunk(dst, N), "dst_r": padded(dst, CHUNKS * P, N).reshape(P, CHUNKS),
        "type_c": by_chunk(edge_type_16, 0), "efT": padded(np.asarray(edge_attr_32).T, (SUPERS + 2) * SUPER, 0),
        "W1": L0_gnn_W1, "b1": np.asarray(L0_gnn_b1).reshape(2, P).T, "W2": L0_gnn_W2, "b2": row(L0_gnn_b2),
        "mW1": L1_gnn_mW1, "mb1": row(L1_gnn_mb1), "mW2T": np.asarray(L1_gnn_mW2).T, "mb2": column(L1_gnn_mb2),
        "uW1": L1_gnn_uW1, "ub1": column(L1_gnn_ub1), "uW2": L1_gnn_uW2, "ub2": row(L1_gnn_ub2),
        "Wl1": L2_gnn_Wl1, "Wr1": L2_gnn_Wr1, "sb1": row(L2_gnn_b1), "gamma": column(L2_gnn_gamma1),
        "beta": column(L2_gnn_beta1), "Wl2": L2_gnn_Wl2, "Wr2": L2_gnn_Wr2, "sb2": row(L2_gnn_b2),
        "Wrel": np.asarray(L3_gnn_weight).transpose(1, 0, 2).reshape(D, R * D),
    }
    arrays = {name: np.ascontiguousarray(a) for name, a in arrays.items()}
    nc = bacc.Bacc("TRN2", target_bir_lowering=False, num_devices=1)
    args = [nc.dram_tensor(f"in_{name}", a.shape, mybir.dt.from_np(a.dtype), kind="ExternalInput").ap()
            for name, a in arrays.items()]
    out = nc.dram_tensor("out", (N, D), F32, kind="ExternalOutput").ap()
    gnn_kernel(nc, *args, out)
    r = run_bass_kernel_spmd(nc, [{f"in_{name}": a for name, a in arrays.items()}], core_ids=[0])
    return r.results[0]["out"]
```
